# Optimizing a Trainium2 kernel written in Bass

```python
import numpy as np
import jax
import jax.numpy as jnp

def _softmax(x, axis=-1):
    return jax.nn.softmax(x, axis=axis)

def _gelu(x):
    return jax.nn.gelu(x, approximate=True)

def _silu(x):
    return jax.nn.silu(x)

def _sigmoid(x):
    return jax.nn.sigmoid(x)

def _layernorm(x, axis=-1, eps=1e-05):
    m = jnp.mean(x, axis=axis, keepdims=True)
    v = jnp.var(x, axis=axis, keepdims=True)
    return (x - m) / jnp.sqrt(v + eps)

def _scatter_add(tgt, idx, src, axis=0):
    return tgt.at[idx].add(src)

def _segment_sum(src, seg, n):
    return jax.ops.segment_sum(src, seg, n)
kernel_name = 'mk_dlrm_tower_d1_rec_r8_1a981c'

def setup_inputs(seed: int=0):
    np.random.seed(seed)
    _w = jnp.asarray

    def _rec_inputs():
        import jax
        import jax.numpy as jnp
        _tk = jax.random.key(seed)
        dense_ctx = jax.random.normal(jax.random.fold_in(_tk, 190), (2048, 16), jnp.float32)
        ids = jnp.stack([jax.random.randint(jax.random.fold_in(_tk, 200 + f), (2048,), 0, v, jnp.int32) for f, v in enumerate([125000, 1000, 12500, 12500, 1000, 12500, 12500, 12500, 1000, 1250, 12500, 1250, 1250, 12500, 1250, 125000, 125000, 1000, 1000, 1000, 12500, 1250, 125000, 12500, 1250, 125000, 125000, 1000, 12500, 1000, 1000, 1000, 1250, 1250, 1000, 1250, 1250, 12500, 1000, 1250])], axis=1)
        tbl_0 = 0.05 * jax.random.normal(jax.random.fold_in(_tk, 500 + 0), (125000, 32), jnp.float32)
        tbl_1 = 0.05 * jax.random.normal(jax.random.fold_in(_tk, 500 + 1), (1000, 32), jnp.float32)
        tbl_2 = 0.05 * jax.random.normal(jax.random.fold_in(_tk, 500 + 2), (12500, 32), jnp.float32)
        tbl_3 = 0.05 * jax.random.normal(jax.random.fold_in(_tk, 500 + 3), (12500, 32), jnp.float32)
        tbl_4 = 0.05 * jax.random.normal(jax.random.fold_in(_tk, 500 + 4), (1000, 32), jnp.float32)
        tbl_5 = 0.05 * jax.random.normal(jax.random.fold_in(_tk, 500 + 5), (12500, 32), jnp.float32)
        tbl_6 = 0.05 * jax.random.normal(jax.random.fold_in(_tk, 500 + 6), (12500, 32), jnp.float32)
        tbl_7 = 0.05 * jax.random.normal(jax.random.fold_in(_tk, 500 + 7), (12500, 32), jnp.float32)
        tbl_8 = 0.05 * jax.random.normal(jax.random.fold_in(_tk, 500 + 8), (1000, 32), jnp.float32)
        tbl_9 = 0.05 * jax.random.normal(jax.random.fold_in(_tk, 500 + 9), (1250, 32), jnp.float32)
        tbl_10 = 0.05 * jax.random.normal(jax.random.fold_in(_tk, 500 + 10), (12500, 32), jnp.float32)
        tbl_11 = 0.05 * jax.random.normal(jax.random.fold_in(_tk, 500 + 11), (1250, 32), jnp.float32)
        tbl_12 = 0.05 * jax.random.normal(jax.random.fold_in(_tk, 500 + 12), (1250, 32), jnp.float32)
        tbl_13 = 0.05 * jax.random.normal(jax.random.fold_in(_tk, 500 + 13), (12500, 32), jnp.float32)
        tbl_14 = 0.05 * jax.random.normal(jax.random.fold_in(_tk, 500 + 14), (1250, 32), jnp.float32)
        tbl_15 = 0.05 * jax.random.normal(jax.random.fold_in(_tk, 500 + 15), (125000, 32), jnp.float32)
        tbl_16 = 0.05 * jax.random.normal(jax.random.fold_in(_tk, 500 + 16), (125000, 32), jnp.float32)
        tbl_17 = 0.05 * jax.random.normal(jax.random.fold_in(_tk, 500 + 17), (1000, 32), jnp.float32)
        tbl_18 = 0.05 * jax.random.normal(jax.random.fold_in(_tk, 500 + 18), (1000, 32), jnp.float32)
        tbl_19 = 0.05 * jax.random.normal(jax.random.fold_in(_tk, 500 + 19), (1000, 32), jnp.float32)
        tbl_20 = 0.05 * jax.random.normal(jax.random.fold_in(_tk, 500 + 20), (12500, 32), jnp.float32)
        tbl_21 = 0.05 * jax.random.normal(jax.random.fold_in(_tk, 500 + 21), (1250, 32), jnp.float32)
        tbl_22 = 0.05 * jax.random.normal(jax.random.fold_in(_tk, 500 + 22), (125000, 32), jnp.float32)
        tbl_23 = 0.05 * jax.random.normal(jax.random.fold_in(_tk, 500 + 23), (12500, 32), jnp.float32)
        tbl_24 = 0.05 * jax.random.normal(jax.random.fold_in(_tk, 500 + 24), (1250, 32), jnp.float32)
        tbl_25 = 0.05 * jax.random.normal(jax.random.fold_in(_tk, 500 + 25), (125000, 32), jnp.float32)
        tbl_26 = 0.05 * jax.random.normal(jax.random.fold_in(_tk, 500 + 26), (125000, 32), jnp.float32)
        tbl_27 = 0.05 * jax.random.normal(jax.random.fold_in(_tk, 500 + 27), (1000, 32), jnp.float32)
        tbl_28 = 0.05 * jax.random.normal(jax.random.fold_in(_tk, 500 + 28), (12500, 32), jnp.float32)
        tbl_29 = 0.05 * jax.random.normal(jax.random.fold_in(_tk, 500 + 29), (1000, 32), jnp.float32)
        tbl_30 = 0.05 * jax.random.normal(jax.random.fold_in(_tk, 500 + 30), (1000, 32), jnp.float32)
        tbl_31 = 0.05 * jax.random.normal(jax.random.fold_in(_tk, 500 + 31), (1000, 32), jnp.float32)
        tbl_32 = 0.05 * jax.random.normal(jax.random.fold_in(_tk, 500 + 32), (1250, 32), jnp.float32)
        tbl_33 = 0.05 * jax.random.normal(jax.random.fold_in(_tk, 500 + 33), (1250, 32), jnp.float32)
        tbl_34 = 0.05 * jax.random.normal(jax.random.fold_in(_tk, 500 + 34), (1000, 32), jnp.float32)
        tbl_35 = 0.05 * jax.random.normal(jax.random.fold_in(_tk, 500 + 35), (1250, 32), jnp.float32)
        tbl_36 = 0.05 * jax.random.normal(jax.random.fold_in(_tk, 500 + 36), (1250, 32), jnp.float32)
        tbl_37 = 0.05 * jax.random.normal(jax.random.fold_in(_tk, 500 + 37), (12500, 32), jnp.float32)
        tbl_38 = 0.05 * jax.random.normal(jax.random.fold_in(_tk, 500 + 38), (1000, 32), jnp.float32)
        tbl_39 = 0.05 * jax.random.normal(jax.random.fold_in(_tk, 500 + 39), (1250, 32), jnp.float32)
        _rk = jax.random.fold_in(_tk, 7)
        W_top1 = 0.0354441 * jax.random.normal(jax.random.fold_in(_tk, 801), (796, 512), jnp.float32)
        W_top2 = 0.0441942 * jax.random.normal(jax.random.fold_in(_tk, 802), (512, 256), jnp.float32)
        W_top3 = 0.0625 * jax.random.normal(jax.random.fold_in(_tk, 803), (256, 1), jnp.float32)
        b_top1 = jnp.zeros((512,), jnp.float32)
        b_top2 = jnp.zeros((256,), jnp.float32)
        return (dense_ctx, ids, tbl_0, tbl_1, tbl_2, tbl_3, tbl_4, tbl_5, tbl_6, tbl_7, tbl_8, tbl_9, tbl_10, tbl_11, tbl_12, tbl_13, tbl_14, tbl_15, tbl_16, tbl_17, tbl_18, tbl_19, tbl_20, tbl_21, tbl_22, tbl_23, tbl_24, tbl_25, tbl_26, tbl_27, tbl_28, tbl_29, tbl_30, tbl_31, tbl_32, tbl_33, tbl_34, tbl_35, tbl_36, tbl_37, tbl_38, tbl_39, W_top1, b_top1, W_top2, b_top2, W_top3)
    dense_ctx, ids, tbl_0, tbl_1, tbl_2, tbl_3, tbl_4, tbl_5, tbl_6, tbl_7, tbl_8, tbl_9, tbl_10, tbl_11, tbl_12, tbl_13, tbl_14, tbl_15, tbl_16, tbl_17, tbl_18, tbl_19, tbl_20, tbl_21, tbl_22, tbl_23, tbl_24, tbl_25, tbl_26, tbl_27, tbl_28, tbl_29, tbl_30, tbl_31, tbl_32, tbl_33, tbl_34, tbl_35, tbl_36, tbl_37, tbl_38, tbl_39, W_top1, b_top1, W_top2, b_top2, W_top3 = _rec_inputs()

    def _L0_rec_setup():
        import jax, jax.numpy as jnp
        import numpy as np
        NUM_FIELDS = 40
        _I_IDX, _J_IDX = np.triu_indices(NUM_FIELDS, k=1)
        key = jax.random.key(seed)
        k1, k2 = jax.random.split(key)
        batch, num_fields, embed_dim = (1024, NUM_FIELDS, 32)
        num_interactions = num_fields * (num_fields - 1) // 2
        embeddings = jax.random.normal(k1, (batch, num_fields, embed_dim), dtype=jnp.float32)
        W = jax.random.normal(k2, (num_interactions, embed_dim, embed_dim), dtype=jnp.float32)
        return {'embeddings': embeddings, 'W': W}
    _L0_rec_all = _L0_rec_setup()
    _L0_rec_in = {k: v for k, v in _L0_rec_all.items() if k in ('W',)}
    del _L0_rec_all
    return {'dense_ctx': dense_ctx, 'ids': ids, 'tbl_0': tbl_0, 'tbl_1': tbl_1, 'tbl_2': tbl_2, 'tbl_3': tbl_3, 'tbl_4': tbl_4, 'tbl_5': tbl_5, 'tbl_6': tbl_6, 'tbl_7': tbl_7, 'tbl_8': tbl_8, 'tbl_9': tbl_9, 'tbl_10': tbl_10, 'tbl_11': tbl_11, 'tbl_12': tbl_12, 'tbl_13': tbl_13, 'tbl_14': tbl_14, 'tbl_15': tbl_15, 'tbl_16': tbl_16, 'tbl_17': tbl_17, 'tbl_18': tbl_18, 'tbl_19': tbl_19, 'tbl_20': tbl_20, 'tbl_21': tbl_21, 'tbl_22': tbl_22, 'tbl_23': tbl_23, 'tbl_24': tbl_24, 'tbl_25': tbl_25, 'tbl_26': tbl_26, 'tbl_27': tbl_27, 'tbl_28': tbl_28, 'tbl_29': tbl_29, 'tbl_30': tbl_30, 'tbl_31': tbl_31, 'tbl_32': tbl_32, 'tbl_33': tbl_33, 'tbl_34': tbl_34, 'tbl_35': tbl_35, 'tbl_36': tbl_36, 'tbl_37': tbl_37, 'tbl_38': tbl_38, 'tbl_39': tbl_39, 'W_top1': W_top1, 'b_top1': b_top1, 'W_top2': W_top2, 'b_top2': b_top2, 'W_top3': W_top3, 'L0_rec_W': _L0_rec_in['W']}

def reference(dense_ctx, ids, tbl_0, tbl_1, tbl_2, tbl_3, tbl_4, tbl_5, tbl_6, tbl_7, tbl_8, tbl_9, tbl_10, tbl_11, tbl_12, tbl_13, tbl_14, tbl_15, tbl_16, tbl_17, tbl_18, tbl_19, tbl_20, tbl_21, tbl_22, tbl_23, tbl_24, tbl_25, tbl_26, tbl_27, tbl_28, tbl_29, tbl_30, tbl_31, tbl_32, tbl_33, tbl_34, tbl_35, tbl_36, tbl_37, tbl_38, tbl_39, W_top1, b_top1, W_top2, b_top2, W_top3, L0_rec_W):
    import jax
    import jax.numpy as jnp

    def _L0_rec_ref(embeddings, W):
        import jax, jax.numpy as jnp
        import numpy as np
        NUM_FIELDS = 40
        _I_IDX, _J_IDX = np.triu_indices(NUM_FIELDS, k=1)
        vi = embeddings[:, _I_IDX, :]
        vj = embeddings[:, _J_IDX, :]
        return jnp.einsum('bke,kef,bkf->bk', vi, W, vj)
    e = jnp.stack([tbl_0[ids[:, 0]], tbl_1[ids[:, 1]], tbl_2[ids[:, 2]], tbl_3[ids[:, 3]], tbl_4[ids[:, 4]], tbl_5[ids[:, 5]], tbl_6[ids[:, 6]], tbl_7[ids[:, 7]], tbl_8[ids[:, 8]], tbl_9[ids[:, 9]], tbl_10[ids[:, 10]], tbl_11[ids[:, 11]], tbl_12[ids[:, 12]], tbl_13[ids[:, 13]], tbl_14[ids[:, 14]], tbl_15[ids[:, 15]], tbl_16[ids[:, 16]], tbl_17[ids[:, 17]], tbl_18[ids[:, 18]], tbl_19[ids[:, 19]], tbl_20[ids[:, 20]], tbl_21[ids[:, 21]], tbl_22[ids[:, 22]], tbl_23[ids[:, 23]], tbl_24[ids[:, 24]], tbl_25[ids[:, 25]], tbl_26[ids[:, 26]], tbl_27[ids[:, 27]], tbl_28[ids[:, 28]], tbl_29[ids[:, 29]], tbl_30[ids[:, 30]], tbl_31[ids[:, 31]], tbl_32[ids[:, 32]], tbl_33[ids[:, 33]], tbl_34[ids[:, 34]], tbl_35[ids[:, 35]], tbl_36[ids[:, 36]], tbl_37[ids[:, 37]], tbl_38[ids[:, 38]], tbl_39[ids[:, 39]]], axis=1)
    z = _L0_rec_ref(e, L0_rec_W)
    z = z.reshape(z.shape[0], -1)
    h = jnp.concatenate([z, dense_ctx], axis=1)
    h = jnp.maximum(h @ W_top1 + b_top1, 0.0)
    h = jnp.maximum(h @ W_top2 + b_top2, 0.0)
    y = h @ W_top3
    return y

_drawn_inputs = setup_inputs


def setup_inputs(seed=0):
    import zlib

    import numpy as np

    out = dict(_drawn_inputs(seed))
    spreads = {'b_top1': (0.0, 0.1), 'b_top2': (0.0, 0.1)}
    factors = {}
    for name, (base, spread) in spreads.items():
        noise = np.random.default_rng([zlib.crc32(name.encode()), seed]).standard_normal(out[name].shape)
        drawn = base * np.exp(spread * noise) if base else spread * noise
        out[name] = jnp.asarray(drawn.astype(out[name].dtype))
    for name, factor in factors.items():
        out[name] = (out[name] * factor).astype(out[name].dtype)
    return out
```

```python
from contextlib import ExitStack

import numpy as np

import concourse.bass as bass
from concourse import mybir

P = 128
B = 2048
F = 40
D = 32
NS = 4
N = B // NS
NT = N // P
GS = P // D
NG = F // GS
OHG = 4
GG = NG - OHG
PV = 125
SLOT = 4
SPT = D // SLOT
STEPS = [(ga, gb) for gb in range(NG) for ga in range(gb + 1)]
ROW = [gb * (gb + 1) // 2 for gb in range(NG + 1)]
KT = (len(STEPS) + SPT - 1) // SPT
WIDTH = [P if ga != gb else 2 * D for ga, gb in STEPS]
WOFF = [sum(WIDTH[:j]) for j in range(len(STEPS) + 1)]
UNITS = [2 if ga != gb else 1 for ga, gb in STEPS]
UOFF = [sum(UNITS[:j]) for j in range(len(STEPS) + 1)]
NU = UOFF[-1]
H1, H2 = 512, 256
RING = 3
PR = 4
OR = 6
DENSE = 16
SELW = D + (SPT - 1) * SLOT
WCH = [0, ROW[4], ROW[6], ROW[8], ROW[9], ROW[10]]

ALU = mybir.AluOpType
ACT = mybir.ActivationFunctionType
F32, BF16, F16, I32 = mybir.dt.float32, mybir.dt.bfloat16, mybir.dt.float16, mybir.dt.int32

MLP_AT = [(0, 8), (8, 13), (13, 19), (20, 26), (26, 34), (34, 38), (38, 42)]
MLP_K = [KT] * (H1 // P) + [H1 // P] * (H2 // P) + [H2 // P]
NM = len(MLP_K)


def mlp_at(j):
    return [(t, k) for t, (a, b) in enumerate(MLP_AT) for k in range(MLP_K[t])
            if a + k * (b - a) // MLP_K[t] == j]


def turn_at(j):
    return next((g for g in range(OHG, NG) if ROW[g] - 2 == j), None)


def z_tile_done(j):
    return j // SPT if j % SPT == SPT - 1 or j == len(STEPS) - 1 else None


def build(nc, vocab, ids_oh, ids_g, ctxT, w_pairs, w1, w2, vecs, consts, tables, scratch, out):
    kts = [vocab[g * GS] // PV for g in range(OHG)]
    KTM = max(kts)
    OHSTEPS = sum(kts)
    assert all(v == kts[i // GS] * PV for i, v in enumerate(vocab[:OHG * GS]))

    with ExitStack() as ctx:
        def sb(name, shape, dt):
            return ctx.enter_context(nc.sbuf_tensor(name, shape, dt))

        def sem(name):
            return ctx.enter_context(nc.semaphore(name))

        ring = ctx.enter_context(nc.psum_tensor("ring", [P, RING, 2, N], F32))
        zbank = ctx.enter_context(nc.psum_tensor("zbank", [P, N], F32))
        misc = ctx.enter_context(nc.psum_tensor("misc", [P, N], F32))

        wp = sb("wp", [P, WOFF[-1]], F32)
        w1s = sb("w1s", [P, KT, H1], F32)
        w2s = sb("w2s", [P, H1 // P, H2], F32)
        vec = sb("vec", [P, 8], F32)
        con = sb("con", [P, consts.shape[1]], F32)
        enat = sb("enat", [P, GG, NT, P], F32)
        eT = sb("eT", [P, NG, N], F32)
        idx = sb("idx", [P, GG, NT, GS], I32)
        idraw = sb("idraw", [P, OHG * GS * B // P], I32)
        idhalf = sb("idhalf", [P, OHG * GS * B // P], F16)
        idb = sb("idb", [P, OHG, GS, N], F16)
        hot = sb("hot", [P, OR, GS, N], BF16)
        tsplit = [sb(f"tsplit{g}", [P, 3, GS, kts[g], D], BF16) for g in range(OHG)]
        prod = sb("prod", [P, PR, 2, N], F32)
        zcur = sb("zcur", [P, KT, N], F32)
        zprev = sb("zprev", [P, KT, N], F32)
        h1 = sb("h1", [P, H1 // P, N], F32)
        h2 = sb("h2", [P, H2 // P, N], F32)
        yrow = sb("yrow", [1, N], F32)
        dense = sb("dense", [DENSE, N], F32)

        def stage(g):
            w = GS * kts[g] * D
            return zprev[:].rearrange("p k n -> p (k n)")[0:PV, (g % 2) * GS * KTM * D:][:, 0:w]\
                .rearrange("p (f k d) -> p f k d", f=GS, d=D)

        def rest(g):
            w = GS * kts[g] * D
            return zcur[:].rearrange("p k n -> p (k n)")[0:PV, 0:w].rearrange("p (f k d) -> p f k d", f=GS, d=D)

        sel = con[:, 0:SELW]
        dsel = con[0:DENSE, SELW:SELW + GS * D]
        c0 = SELW + GS * D
        vcol = [con[:, c0 + g * KTM:c0 + (g + 1) * KTM] for g in range(OHG)]
        ident = con[:, c0 + OHG * KTM:c0 + OHG * KTM + P]
        b1c, b2c, w3c = vec[:, 0:4], vec[:, 4:6], vec[:, 6:8]

        idraw_in = sem("idraw_in")
        idhalf_ready = sem("idhalf_ready")
        idhalf_out = sem("idhalf_out")
        con_in = sem("con_in")
        vec_in = sem("vec_in")
        wp_in = [sem(f"wp_in{c}") for c in range(len(WCH) - 1)]
        w1_in = sem("w1_in")
        w2_in = sem("w2_in")
        table_in = [sem(f"table_in{g}") for g in range(OHG)]
        part_hi = sem("part_hi")
        part_rest = sem("part_rest")
        part_mid = sem("part_mid")
        part_lo = sem("part_lo")
        idb_in = [sem(f"idb_in{g}") for g in range(OHG)]
        idx_in = [sem(f"idx_in{g}") for g in range(GG)]
        gathered = [sem(f"gathered{g}") for g in range(GG)]
        dense_in = sem("dense_in")
        hot_ready = sem("hot_ready")
        hot_used = sem("hot_used")
        turned = sem("turned")
        mlp_ready = sem("mlp_ready")
        et_ready = sem("et_ready")
        mlp_ev = sem("mlp_ev")
        u_ready = sem("u_ready")
        multiplied = sem("multiplied")
        reduced = sem("reduced")
        z_ev = sem("z_ev")
        zprev_ready = sem("zprev_ready")
        y_stored = sem("y_stored")
        pool_passed = sem("pool_passed")
        pe_passed = sem("pe_passed")

        block = ctx.enter_context(nc.Block())

        def is_first(s):
            return isinstance(s, int) and s == 0

        def wait_apart(eng, s, value, passed):
            eng.wait_ge(s, value)
            eng.sem_inc(passed, 1)

        @block.sync
        def _(sp):
            sp.dma_start(idraw[:], ids_oh).then_inc(idraw_in, 16)
            sp.dma_start(con[:], consts).then_inc(con_in, 16)
            sp.wait_ge(idhalf_ready, 1)
            sp.dma_start(scratch.rearrange("(p n) -> p n", p=P), idhalf[:]).then_inc(idhalf_out, 16)
            sp.wait_ge(idhalf_out, 16)

            def load_ids_broadcast(s):
                for g in range(OHG):
                    src = scratch.rearrange("(g f s n) -> s g f n", g=OHG, f=GS, s=NS)[s, g]
                    sp.dma_start(idb[:, g], src.partition_broadcast(P)).then_inc(idb_in[g], 16)

            load_ids_broadcast(0)
            for c in range(len(WCH) - 1):
                a, b = WOFF[WCH[c]], WOFF[WCH[c + 1]]
                sp.dma_start(wp[:, a:b], w_pairs[:, a:b]).then_inc(wp_in[c], 16)
            sp.dma_start(dense[:], ctxT[0]).then_inc(dense_in, 16)
            sp.dma_start(w1s[:], w1).then_inc(w1_in, 16)
            sp.dma_start(w2s[:], w2).then_inc(w2_in, 16)
            sp.dma_start(vec[:], vecs).then_inc(vec_in, 16)

            with sp.Fori(1, NS) as s:
                sp.wait_ge(hot_ready, s * OHSTEPS)
                load_ids_broadcast(s)
                for g in range(GG):
                    sp.wait_ge(gathered[g], s * (16 * NT * GS))
                    sp.dma_start(idx[:, g], ids_g[s, :, g]).then_inc(idx_in[g], 16)
                sp.wait_ge(reduced, s * NU)
                sp.dma_start(dense[:], ctxT[s]).then_inc(dense_in, 16)

        @block.gpsimd
        def _(pool):
            passed = pool_passed
            def gather_slice(s):
                for g in range(GG):
                    pool.wait_ge(idx_in[g], s * 16 + 16)
                    if not is_first(s):
                        wait_apart(pool, turned, (s - 1) * GG + g + 1, passed)
                    for f in range(GS):
                        for t in range(NT):
                            pool.indirect_dma_start(
                                out=enat[:, g, t, f * D:(f + 1) * D], out_offset=None,
                                in_=tables[(OHG + g) * GS + f],
                                in_offset=bass.IndirectOffsetOnAxis(ap=idx[:, g, t, f:f + 1], axis=0),
                            ).then_inc(gathered[g], 16)

            gather_slice(0)
            with pool.Fori(1, NS) as s:
                gather_slice(s)

        @block.vector
        def _(dve):
            def split_tables(g):
                dve.wait_ge(part_hi, g + 1)
                if g:
                    dve.wait_ge(part_lo, g)
                nc.vector.tensor_tensor(rest(g), stage(g), tsplit[g][0:PV, 0], ALU.subtract).then_inc(part_rest, 1)
                dve.wait_ge(part_mid, g + 1)
                nc.vector.tensor_tensor(tsplit[g][0:PV, 2], rest(g), tsplit[g][0:PV, 1],
                                        ALU.subtract).then_inc(part_lo, 1)

            def build_hot(s):
                n = 0
                for g in range(OHG):
                    dve.wait_ge(idb_in[g], s * 16 + 16)
                    for k in range(kts[g]):
                        if n >= OR:
                            dve.wait_ge(hot_used, s * OHSTEPS + (n - OR + 1))
                        elif n == 0 and not is_first(s):
                            dve.wait_ge(hot_used, s * OHSTEPS)
                        nc.vector.tensor_scalar(hot[0:PV, n % OR], idb[0:PV, g], vcol[g][0:PV, k:k + 1],
                                                None, ALU.is_equal).then_inc(hot_ready, 1)
                        n += 1

            def multiply(s):
                u = 0
                for j, (ga, gb) in enumerate(STEPS):
                    if ga == 0:
                        dve.wait_ge(et_ready, s * NG + gb + 1)
                    for h in range(UNITS[j]):
                        dve.wait_ge(u_ready, s * NU + u + 1)
                        if u >= PR:
                            dve.wait_ge(reduced, s * NU + (u - PR + 1))
                        elif u == 0 and not is_first(s):
                            dve.wait_ge(reduced, s * NU)
                        e_b = eT[:, gb:gb + 1, :].to_broadcast([P, 2, N])
                        nc.vector.tensor_tensor(prod[:, u % PR], ring[:, u % RING], e_b,
                                                ALU.mult).then_inc(multiplied, 1)
                        u += 1

            dve.wait_ge(idraw_in, 16)
            nc.vector.tensor_copy(idhalf[:], idraw[:]).then_inc(idhalf_ready, 1)
            for g in range(OHG):
                split_tables(g)
            dve.wait_ge(con_in, 16)
            build_hot(0)
            multiply(0)
            with dve.Fori(1, NS) as s:
                build_hot(s)
                multiply(s)

        @block.scalar
        def _(act):
            def take_group(g):
                nc.scalar.activation(eT[:, g], misc[:], ACT.Copy).then_inc(et_ready, 1)

            def take_mlp(t, done, src):
                act.wait_ge(mlp_ready, done + t + 1)
                if t < H1 // P:
                    nc.scalar.activation(h1[:, t], src, ACT.Relu, bias=b1c[:, t:t + 1]).then_inc(mlp_ev, 1)
                elif t < NM - 1:
                    m = t - H1 // P
                    nc.scalar.activation(h2[:, m], src, ACT.Relu, bias=b2c[:, m:m + 1]).then_inc(mlp_ev, 1)
                else:
                    nc.scalar.activation(yrow[:], src[0:1], ACT.Copy).then_inc(mlp_ev, 1)

            def store_y(s):
                act.wait_ge(mlp_ev, s * NM + NM)
                act.dma_start(out[s], yrow[:]).then_inc(y_stored, 16)

            def slice_copies(s):
                n = 0
                for g in range(OHG):
                    n += kts[g]
                    act.wait_ge(hot_used, s * OHSTEPS + n)
                    take_group(g)
                for j in range(len(STEPS) + 1):
                    g = turn_at(j)
                    if g is not None:
                        act.wait_ge(turned, s * GG + (g - OHG + 1))
                        take_group(g)
                    k = z_tile_done(j - 1) if j else None
                    if k is not None:
                        act.wait_ge(reduced, s * NU + UOFF[j])
                        nc.scalar.activation(zcur[:, k], zbank[:], ACT.Copy).then_inc(z_ev, 1)
                    if not is_first(s):
                        for t, k in mlp_at(j):
                            if k == MLP_K[t] - 1:
                                take_mlp(t, (s - 1) * NM, misc[:])
                                if t == NM - 1:
                                    store_y(s - 1)
                if not is_first(s):
                    act.wait_ge(y_stored, s * 16)
                act.wait_ge(z_ev, s * KT + KT)
                nc.scalar.activation(zprev[:], zcur[:], ACT.Copy).then_inc(zprev_ready, 1)

            for g in range(GG):
                act.dma_start(idx[:, g], ids_g[0, :, g]).then_inc(idx_in[g], 16)
            for g in range(OHG):
                if g >= 2:
                    act.wait_ge(part_rest, g - 1)
                for f in range(GS):
                    act.dma_start(stage(g)[:, f], tables[g * GS + f].rearrange("(p k) d -> p k d", k=kts[g]))\
                       .then_inc(table_in[g], 16)
                if g >= 1:
                    split_parts = [g - 1] if g < OHG - 1 else [g - 1, g]
                else:
                    split_parts = []
                for q in split_parts:
                    act.wait_ge(table_in[q], 16 * GS)
                    nc.scalar.activation(tsplit[q][0:PV, 0], stage(q), ACT.Copy).then_inc(part_hi, 1)
                    act.wait_ge(part_rest, q + 1)
                    nc.scalar.activation(tsplit[q][0:PV, 1], rest(q), ACT.Copy).then_inc(part_mid, 1)
            act.wait_ge(vec_in, 16)
            slice_copies(0)
            with act.Fori(1, NS) as s:
                slice_copies(s)
            for t in range(NM):
                take_mlp(t, (NS - 1) * NM, ring[:, t % RING, 0])
            store_y(NS - 1)
            act.wait_ge(y_stored, NS * 16)

        @block.tensor
        def _(pe):
            passed = pe_passed

            def look_up(s):
                n = 0
                for g in range(OHG):
                    if g or not is_first(s):
                        pe.wait_ge(et_ready, s * NG + g)
                    if is_first(s):
                        pe.wait_ge(part_lo, g + 1)
                    for k in range(kts[g]):
                        pe.wait_ge(hot_ready, s * OHSTEPS + n + 1)
                        for part in range(3):
                            for f in range(GS):
                                mm = nc.tensor.matmul(misc[f * D:(f + 1) * D], tsplit[g][0:PV, part, f, k],
                                                      hot[0:PV, n % OR, f], start=(k == 0 and part == 0),
                                                      stop=(k == kts[g] - 1 and part == 2))
                        mm.then_inc(hot_used, 1)
                        n += 1

            def turn(s, g):
                pe.wait_ge(gathered[g - OHG], s * (16 * NT * GS) + 16 * NT * GS)
                tiles = [t for t in range(NM) if MLP_AT[t][1] <= ROW[g] - 2]
                if is_first(s):
                    pe.wait_ge(et_ready, g)
                else:
                    pe.wait_ge(et_ready, s * NG + g)
                    pe.wait_ge(mlp_ev, (s - 1) * NM + len(tiles))
                for t in range(NT):
                    mm = nc.tensor.transpose(misc[:, t * P:(t + 1) * P], enat[:, g - OHG, t], ident)
                mm.then_inc(turned, 1)

            def unit_is_free(s, u, apart=False):
                if u < RING and (u or is_first(s)):
                    return
                count = s * NU + (u - RING + 1 if u else 0)
                if apart and not is_first(s):
                    wait_apart(pe, multiplied, count, passed)
                else:
                    pe.wait_ge(multiplied, count)

            def make_u(s, j):
                ga, gb = STEPS[j]
                if ga == 0:
                    pe.wait_ge(et_ready, s * NG + gb + 1)
                if is_first(s) and j in WCH:
                    pe.wait_ge(wp_in[WCH.index(j)], 16)
                u = UOFF[j]
                if ga != gb:
                    for h in range(2):
                        unit_is_free(s, u + h)
                        for i in range(2):
                            a = 2 * h + i
                            rows = slice(a * D, (a + 1) * D)
                            mm = nc.tensor.matmul(ring[:, (u + h) % RING, i], wp[rows, WOFF[j]:WOFF[j] + P],
                                                  eT[rows, ga], start=True, stop=True)
                        mm.then_inc(u_ready, 1)
                else:
                    unit_is_free(s, u, apart=True)
                    for i in range(2):
                        for q in range(GS):
                            r = (q + 1 + i) % GS
                            rows = slice(r * D, (r + 1) * D)
                            mm = nc.tensor.matmul(ring[q * D:(q + 1) * D, u % RING, i],
                                                  wp[rows, WOFF[j] + i * D:WOFF[j] + (i + 1) * D],
                                                  eT[rows, ga], start=True, stop=True)
                    mm.then_inc(u_ready, 1)

            def reduce(s, j):
                ga, gb = STEPS[j]
                k, m = j // SPT, j % SPT
                pick = sel[:, SELW - D - m * SLOT:SELW - m * SLOT]
                if m == 0 and (k or not is_first(s)):
                    pe.wait_ge(z_ev, s * KT + k)
                in_tile = range(k * SPT, j)
                last = z_tile_done(j) is not None
                if last and k == KT - 1:
                    if is_first(s):
                        pe.wait_ge(dense_in, 16)
                    else:
                        wait_apart(pe, dense_in, s * 16 + 16, passed)
                    for a in range(GS):
                        nc.tensor.matmul(zbank[a * D:(a + 1) * D], dsel[:, a * D:(a + 1) * D], dense[:],
                                         start=False, stop=(ga == gb and a >= 2), skip_group_check=True)
                u = UOFF[j]
                if ga != gb:
                    for h in range(2):
                        pe.wait_ge(multiplied, s * NU + u + h + 1)
                        for i in range(2):
                            a = 2 * h + i
                            fresh = m == 0 or (a >= 2 and all(STEPS[q][0] == STEPS[q][1] for q in in_tile))
                            mm = nc.tensor.matmul(zbank[a * D:(a + 1) * D], pick, prod[:, (u + h) % PR, i],
                                                  start=fresh, stop=last, skip_group_check=True)
                        mm.then_inc(reduced, 1)
                else:
                    pe.wait_ge(multiplied, s * NU + u + 1)
                    for i, rows in enumerate((P, 2 * D)):
                        mm = nc.tensor.matmul(zbank[i * D:(i + 1) * D], pick[0:rows], prod[0:rows, u % PR, i],
                                              start=(m == 0), stop=last, skip_group_check=True)
                    mm.then_inc(reduced, 1)

            def mlp(s, t, k, dst):
                if t < H1 // P:
                    if t == 0 and k == 0:
                        pe.wait_ge(zprev_ready, s + 1)
                    w, x = w1s[:, k, t * P:(t + 1) * P], zprev[:, k]
                elif t < NM - 1:
                    if k == 0:
                        pe.wait_ge(mlp_ev, s * NM + H1 // P)
                    m = t - H1 // P
                    w, x = w2s[:, k, m * P:(m + 1) * P], h1[:, k]
                else:
                    if k == 0:
                        pe.wait_ge(mlp_ev, s * NM + NM - 1)
                    w, x, dst = w3c[:, k:k + 1], h2[:, k], dst[0:1]
                mm = nc.tensor.matmul(dst, w, x, start=(k == 0), stop=(k == MLP_K[t] - 1))
                if k == MLP_K[t] - 1:
                    mm.then_inc(mlp_ready, 1)

            def slice_steps(s):
                look_up(s)
                make_u(s, 0)
                held_by_group = True
                groups = OHG
                for j in range(len(STEPS)):
                    g = turn_at(j)
                    if g is not None:
                        turn(s, g)
                        held_by_group, groups = True, g + 1
                    if j + 1 < len(STEPS):
                        make_u(s, j + 1)
                    if j:
                        reduce(s, j - 1)
                    if not is_first(s):
                        for t, k in mlp_at(j):
                            if k == 0 and held_by_group:
                                pe.wait_ge(et_ready, s * NG + groups)
                            elif k == 0:
                                pe.wait_ge(mlp_ev, (s - 1) * NM + t)
                            held_by_group = False
                            mlp(s - 1, t, k, misc[:])
                reduce(s, len(STEPS) - 1)

            pe.wait_ge(con_in, 16)
            slice_steps(0)
            pe.wait_ge(w1_in, 16)
            pe.wait_ge(w2_in, 16)
            pe.wait_ge(vec_in, 16)
            with pe.Fori(1, NS) as s:
                slice_steps(s)
            for t in range(NM):
                if t == 0:
                    pe.wait_ge(multiplied, NS * NU)
                if t >= RING:
                    pe.wait_ge(mlp_ev, (NS - 1) * NM + t - RING + 1)
                for k in range(MLP_K[t]):
                    mlp(NS - 1, t, k, ring[:, t % RING, 0])


def field_order(vocab):
    small = sorted((f for f in range(F) if vocab[f] % PV == 0), key=lambda f: (vocab[f], f))[:OHG * GS]
    return small + [f for f in range(F) if f not in small]


def pair_index(i, j):
    return i * (2 * F - i - 1) // 2 + (j - i - 1)


def lay_out_pairs(W, order):
    def mat(src, dst):
        return W[pair_index(src, dst)] if src < dst else W[pair_index(dst, src)].T

    w = np.empty((P, WOFF[-1]), W.dtype)
    for j, (ga, gb) in enumerate(STEPS):
        for a in range(GS):
            rows = slice(a * D, (a + 1) * D)
            src = order[ga * GS + a]
            dests = range(GS) if ga != gb else [(a - 1) % GS, (a - 2) % GS]
            for c, q in enumerate(dests):
                w[rows, WOFF[j] + c * D:WOFF[j] + (c + 1) * D] = mat(src, order[gb * GS + q])
    return w


def top_rows(order):
    rows = np.zeros((P, KT), np.int64)
    for j, (ga, gb) in enumerate(STEPS):
        k, m = j // SPT, j % SPT
        for a in range(GS):
            for q in range(GS):
                if ga != gb:
                    pair = (order[ga * GS + a], order[gb * GS + q])
                elif a == 0 or (a == 1 and q < 2):
                    pair = (order[ga * GS + (q + 1 + a) % GS], order[ga * GS + q])
                else:
                    continue
                rows[a * D + m * SLOT + q, k] = pair_index(min(pair), max(pair))
    for a in range(GS):
        for r in range(SLOT):
            rows[a * D + (SPT - 1) * SLOT + r, KT - 1] = F * (F - 1) // 2 + a * SLOT + r
    return rows


def constants(kts):
    KTM = max(kts)
    sel = np.zeros((P, SELW), np.float32)
    sel[np.arange(P), SELW - D + np.arange(P) // D] = 1
    dsel = np.zeros((P, GS * D), np.float32)
    for r in range(DENSE):
        dsel[r, (r // SLOT) * D + (SPT - 1) * SLOT + r % SLOT] = 1
    vcol = np.zeros((P, len(kts), KTM), np.float32)
    for g, k in enumerate(kts):
        vcol[:, g, :k] = np.arange(P)[:, None] * k + np.arange(k)
    return np.concatenate([sel, dsel, vcol.reshape(P, -1), np.eye(P, dtype=np.float32)], axis=1)


def kernel(dense_ctx, ids, W_top1, b_top1, W_top2, b_top2, W_top3, L0_rec_W, **tables):
    import numpy as _np
    import concourse.bacc as _bacc
    from concourse import mybir as _mybir
    from concourse.bass_utils import run_bass_kernel_spmd as _run

    tabs = [_np.asarray(tables[f"tbl_{f}"]) for f in range(F)]
    order = field_order([t.shape[0] for t in tabs])
    vocab = [tabs[f].shape[0] for f in order]
    kts = [vocab[g * GS] // PV for g in range(OHG)]
    idT = _np.asarray(ids).T[order]
    noh = OHG * GS
    arrays = {
        "ids_oh": idT[:noh].reshape(P, -1),
        "ids_g": idT[noh:].reshape(GG, GS, NS, NT, P).transpose(2, 4, 0, 3, 1),
        "ctxT": _np.asarray(dense_ctx).reshape(NS, N, DENSE).transpose(0, 2, 1),
        "w_pairs": lay_out_pairs(_np.asarray(L0_rec_W), order),
        "w1": _np.asarray(W_top1)[top_rows(order)],
        "w2": _np.asarray(W_top2).reshape(H1 // P, P, H2).transpose(1, 0, 2),
        "vecs": _np.concatenate([_np.asarray(x).reshape(-1, P).T for x in (b_top1, b_top2, W_top3)], axis=1),
        "consts": constants(kts),
    }
    for i, f in enumerate(order):
        arrays[f"table{i}"] = tabs[f]
    arrays = {k: _np.ascontiguousarray(v) for k, v in arrays.items()}

    nc = _bacc.Bacc("TRN2", target_bir_lowering=False, num_devices=1)
    ap = {k: nc.dram_tensor(k, v.shape, _mybir.dt.from_np(v.dtype), kind="ExternalInput").ap()
          for k, v in arrays.items()}
    scratch = nc.dram_tensor("scratch", (noh * B,), F16, kind="Internal").ap()
    out = nc.dram_tensor("y", (NS, 1, N), F32, kind="ExternalOutput").ap()
    build(nc, vocab, ap["ids_oh"], ap["ids_g"], ap["ctxT"], ap["w_pairs"], ap["w1"], ap["w2"], ap["vecs"],
          ap["consts"], [ap[f"table{i}"] for i in range(F)], scratch, out)
    r = _run(nc, [arrays], core_ids=[0])
    return r.results[0]["y"].reshape(B, 1)
```

```python
from contextlib import ExitStack

import numpy as np

import concourse.bass as bass
from concourse import mybir

P = 128
B = 2048
F = 40
D = 32
NS = 4
N = B // NS
NT = N // P
GS = P // D
NG = F // GS
OHG = 2
GG = NG - OHG
PV = 125
SLOT = 4
SPT = D // SLOT
STEPS = [(gs, gd) for gs in range(NG) for gd in range(gs + 1)]
ROW = [g * (g + 1) // 2 for g in range(NG + 1)]
PAIRED = [j for j, (gs, gd) in enumerate(STEPS) if gs != gd]
NQ = len(PAIRED)
KT = (len(STEPS) + SPT - 1) // SPT
UNITS = [2 if gs != gd else 1 for gs, gd in STEPS]
UOFF = [sum(UNITS[:j]) for j in range(len(STEPS) + 1)]
NU = UOFF[-1]
H1, H2 = 512, 256
RING = 3
PR = 4
WR = 5
WC = 4
NWC = (NQ + WC - 1) // WC
STAGES = 3
LEAD = 4
OR = 6
DENSE = 16
SELW = D + (SPT - 1) * SLOT
ALU = mybir.AluOpType
ACT = mybir.ActivationFunctionType
F32, F32R, BF16, F16, I32 = (mybir.dt.float32, mybir.dt.float32r, mybir.dt.bfloat16, mybir.dt.float16,
                             mybir.dt.int32)

MLP_AT = [(6, 11), (11, 17), (17, 24), (24, 32), (32, 36), (36, 41), (42, 46)]
MLP_K = [KT] * (H1 // P) + [H1 // P] * (H2 // P) + [H2 // P]
NM = len(MLP_K)


def mlp_at(j):
    return [(t, k) for t, (a, b) in enumerate(MLP_AT) for k in range(MLP_K[t])
            if a + k * (b - a) // MLP_K[t] == j]


def turn_at(j):
    return next((g for g in range(OHG, NG) if turn_step(g) == j), None)


def turn_step(g):
    return max(ROW[g] - LEAD, 0)


def z_tile_done(j):
    return j // SPT if j % SPT == SPT - 1 or j == len(STEPS) - 1 else None


def build(nc, vocab, ids_oh, ids_g, ctxT, w_pairs, w_own, w1, w2, vecs, consts, tables, scratch,
          w_parts, out):
    kts = [vocab[g * GS] // PV for g in range(OHG)]
    KTM = max(kts)
    OHSTEPS = sum(kts)
    assert all(v == kts[i // GS] * PV for i, v in enumerate(vocab[:OHG * GS]))

    with ExitStack() as ctx:
        def sb(name, shape, dt):
            return ctx.enter_context(nc.sbuf_tensor(name, shape, dt))

        def sem(name):
            return ctx.enter_context(nc.semaphore(name))

        ring = ctx.enter_context(nc.psum_tensor("ring", [P, RING, 2, N], F32))
        zbank = ctx.enter_context(nc.psum_tensor("zbank", [P, N], F32))
        misc = ctx.enter_context(nc.psum_tensor("misc", [P, N], F32))

        wst = sb("wst", [P, WR, GS, P], F32R)
        wown = sb("wown", [P, NG, 2, D], F32)
        stack = sb("stack", [P, 2, GS, N], F32R)
        ehi = sb("ehi", [P, N], F32R)
        elo = sb("elo", [P, N], F32R)
        w1s = sb("w1s", [P, KT, H1], F32)
        w2s = sb("w2s", [P, H1 // P, H2], F32)
        vec = sb("vec", [P, 8], F32)
        con = sb("con", [P, consts.shape[1]], F32)
        enat = sb("enat", [P, GG, NT, P], F32)
        eT = sb("eT", [P, NG, N], F32)
        idx = sb("idx", [P, GG, NT, GS], I32)
        idraw = sb("idraw", [P, OHG * GS * B // P], I32)
        idhalf = sb("idhalf", [P, OHG * GS * B // P], F16)
        idb = sb("idb", [P, OHG, GS, N], F16)
        hot = sb("hot", [P, OR, GS, N], BF16)
        tsplit = [sb(f"tsplit{g}", [P, 3, GS, kts[g], D], BF16) for g in range(OHG)]
        prod = sb("prod", [P, PR, 2, N], F32)
        zcur = sb("zcur", [P, KT, N], F32)
        zprev = sb("zprev", [P, KT, N], F32)
        h1 = sb("h1", [P, H1 // P, N], F32)
        h2 = sb("h2", [P, H2 // P, N], F32)
        yrow = sb("yrow", [1, N], F32)
        dense = sb("dense", [DENSE, N], F32)

        def stage(g):
            return h1[:].rearrange("p k n -> p (k n)")[0:PV, (g % 2) * GS * KTM * D:(g % 2 + 1) * GS * KTM * D]\
                .rearrange("p (f k d) -> p f k d", f=GS, d=D)

        def rest(g):
            return h2[:].rearrange("p k n -> p (k n)")[0:PV, 0:GS * KTM * D].rearrange("p (f k d) -> p f k d", f=GS, d=D)

        def w_raw(c):
            i = c % (2 * PR)
            return prod[:, i // 2, i % 2, 0:P * w_steps(c)]

        def w_part(c, part):
            return zprev[:, part * STAGES + c % STAGES, 0:P * w_steps(c)]

        def w_steps(c):
            return min(WC, NQ - c * WC)

        sel = con[:, 0:SELW]
        dsel = con[0:DENSE, SELW:SELW + GS * D]
        c0 = SELW + GS * D
        vcol = [con[:, c0 + g * KTM:c0 + (g + 1) * KTM] for g in range(OHG)]
        ident = con[:, c0 + OHG * KTM:c0 + OHG * KTM + P]
        b1c, b2c, w3c = vec[:, 0:4], vec[:, 4:6], vec[:, 6:8]

        idraw_in = sem("idraw_in")
        idhalf_ready = sem("idhalf_ready")
        idhalf_out = sem("idhalf_out")
        con_in = sem("con_in")
        vec_in = sem("vec_in")
        wraw_in = [sem(f"wraw_in{c}") for c in range(NWC)]
        w_hi = sem("w_hi")
        w_lo = sem("w_lo")
        w_out = [sem(f"w_out{c}") for c in range(NWC)]
        w_in = [sem(f"w_in{i}") for i in range(WR)]
        wown_in = sem("wown_in")
        stack_in = [sem("stack_in_even"), sem("stack_in_odd")]
        elo_ready = sem("elo_ready")
        w1_in = sem("w1_in")
        w2_in = sem("w2_in")
        table_in = [sem(f"table_in{g}") for g in range(OHG)]
        part_hi = sem("part_hi")
        part_rest = sem("part_rest")
        part_mid = sem("part_mid")
        part_lo = sem("part_lo")
        idb_in = [sem(f"idb_in{g}") for g in range(OHG)]
        idx_in = [sem(f"idx_in{g}") for g in range(GG)]
        gathered = [sem(f"gathered{g}") for g in range(GG)]
        dense_in = sem("dense_in")
        hot_ready = sem("hot_ready")
        hot_used = sem("hot_used")
        turned = sem("turned")
        mlp_ready = sem("mlp_ready")
        et_ready = sem("et_ready")
        mlp_ev = sem("mlp_ev")
        u_ready = sem("u_ready")
        multiplied = sem("multiplied")
        reduced = sem("reduced")
        z_ev = sem("z_ev")
        zprev_ready = sem("zprev_ready")
        y_stored = sem("y_stored")
        pool_passed = sem("pool_passed")
        pe_passed = sem("pe_passed")

        block = ctx.enter_context(nc.Block())

        def is_first(s):
            return isinstance(s, int) and s == 0

        def stacks(s, g):
            each = 16 * 4 * GS
            return s * (each * len(range(2 - g % 2, NG, 2))) + each * ((g - 1) // 2 + 1)

        def wait_apart(eng, s, value, passed):
            eng.wait_ge(s, value)
            eng.sem_inc(passed, 1)

        @block.sync
        def _(sp):
            sp.dma_start(idraw[:], ids_oh).then_inc(idraw_in, 16)
            sp.dma_start(con[:], consts).then_inc(con_in, 16)

            def load_raw(c):
                sp.dma_start(w_raw(c), w_pairs[:, c * WC * P:c * WC * P + w_steps(c) * P]).then_inc(wraw_in[c], 16)

            for c in range(min(2 * PR, NWC)):
                load_raw(c)
            sp.wait_ge(idhalf_ready, 1)
            sp.dma_start(scratch.rearrange("(p n) -> p n", p=P), idhalf[:]).then_inc(idhalf_out, 16)
            sp.wait_ge(idhalf_out, 16)

            def load_ids_broadcast(s):
                for g in range(OHG):
                    src = scratch.rearrange("(g f s n) -> s g f n", g=OHG, f=GS, s=NS)[s, g]
                    sp.dma_start(idb[:, g], src.partition_broadcast(P)).then_inc(idb_in[g], 16)

            def build_stacks(s, load_next):
                for g in range(1, NG):
                    sp.wait_ge(elo_ready, s * (NG - 1) + g)
                    for f in range(GS):
                        for i, part in enumerate((ehi, ehi, elo, elo)):
                            sp.dma_start(stack[i * D:(i + 1) * D, g % 2, f].bitcast(F32),
                                         part[f * D:(f + 1) * D].bitcast(F32)).then_inc(stack_in[g % 2], 16)
                    if load_next and g >= OHG:
                        load_indices(s, g)
                if load_next:
                    sp.wait_ge(hot_ready, s * OHSTEPS + OHSTEPS)
                    load_ids_broadcast(s + 1)
                    sp.wait_ge(reduced, s * NU + NU)
                    sp.dma_start(dense[:], ctxT[s + 1]).then_inc(dense_in, 16)

            def load_indices(s, g):
                sp.wait_ge(gathered[g - OHG], s * (16 * NT * GS) + 16 * NT * GS)
                sp.dma_start(idx[:, g - OHG], ids_g[s + 1, :, g - OHG]).then_inc(idx_in[g - OHG], 16)

            load_ids_broadcast(0)
            sp.dma_start(wown[:], w_own).then_inc(wown_in, 16)
            for c in range(NWC):
                sp.wait_ge(w_lo, c + 1)
                for part in range(2):
                    for a in range(GS):
                        sp.dma_start(w_parts[c * WC:c * WC + w_steps(c), part * D:(part + 1) * D, a].rearrange("q e n -> e q n"),
                                     w_part(c, part)[a * D:(a + 1) * D].rearrange("e (q n) -> e q n", n=P)).then_inc(w_out[c], 16)
                if c + 2 * PR < NWC:
                    load_raw(c + 2 * PR)
            sp.dma_start(dense[:], ctxT[0]).then_inc(dense_in, 16)
            sp.dma_start(w1s[:], w1).then_inc(w1_in, 16)
            sp.dma_start(w2s[:], w2).then_inc(w2_in, 16)
            sp.dma_start(vec[:], vecs).then_inc(vec_in, 16)

            build_stacks(0, True)
            with sp.Fori(1, NS - 1) as s:
                build_stacks(s, True)
            build_stacks(NS - 1, False)

        @block.gpsimd
        def _(pool):
            passed = pool_passed
            def gather_slice(s):
                for g in range(GG):
                    pool.wait_ge(idx_in[g], s * 16 + 16)
                    if not is_first(s):
                        wait_apart(pool, turned, (s - 1) * GG + g + 1, passed)
                    for f in range(GS):
                        for t in range(NT):
                            pool.indirect_dma_start(
                                out=enat[:, g, t, f * D:(f + 1) * D], out_offset=None,
                                in_=tables[(OHG + g) * GS + f],
                                in_offset=bass.IndirectOffsetOnAxis(ap=idx[:, g, t, f:f + 1], axis=0),
                            ).then_inc(gathered[g], 16)

            gather_slice(0)
            with pool.Fori(1, NS) as s:
                gather_slice(s)

        @block.vector
        def _(dve):
            def split_tables(g):
                dve.wait_ge(part_hi, g + 1)
                if g:
                    dve.wait_ge(part_lo, g)
                nc.vector.tensor_tensor(rest(g), stage(g), tsplit[g][0:PV, 0], ALU.subtract).then_inc(part_rest, 1)
                dve.wait_ge(part_mid, g + 1)
                nc.vector.tensor_tensor(tsplit[g][0:PV, 2], rest(g), tsplit[g][0:PV, 1],
                                        ALU.subtract).then_inc(part_lo, 1)

            def build_hot(s):
                n = 0
                for g in range(OHG):
                    dve.wait_ge(idb_in[g], s * 16 + 16)
                    for k in range(kts[g]):
                        if n >= OR:
                            dve.wait_ge(hot_used, s * OHSTEPS + (n - OR + 1))
                        elif n == 0 and not is_first(s):
                            dve.wait_ge(hot_used, s * OHSTEPS)
                        nc.vector.tensor_scalar(hot[0:PV, n % OR], idb[0:PV, g], vcol[g][0:PV, k:k + 1],
                                                None, ALU.is_equal).then_inc(hot_ready, 1)
                        n += 1

            def split_w(c):
                dve.wait_ge(w_hi, c + 1)
                if c >= STAGES:
                    dve.wait_ge(w_out[c - STAGES], 16 * 2 * GS)
                nc.vector.tensor_tensor(w_part(c, 1).bitcast(F32R), w_raw(c), w_part(c, 0),
                                        ALU.subtract).then_inc(w_lo, 1)

            def low_parts(s, g):
                dve.wait_ge(et_ready, s * NG + g + 1)
                nc.vector.tensor_tensor(elo[:], eT[:, g], ehi[:].bitcast(F32),
                                        ALU.subtract).then_inc(elo_ready, 1)

            def multiply(s):
                u = 0
                for g in range(1, OHG):
                    low_parts(s, g)
                for j, (gs, gd) in enumerate(STEPS):
                    if turn_at(j - 1) is not None:
                        low_parts(s, turn_at(j - 1))
                    for h in range(UNITS[j]):
                        dve.wait_ge(u_ready, s * NU + u + 1)
                        if u >= PR:
                            dve.wait_ge(reduced, s * NU + (u - PR + 1))
                        elif u == 0 and not is_first(s):
                            dve.wait_ge(reduced, s * NU)
                        e_d = eT[:, gd:gd + 1, :].to_broadcast([P, 2, N])
                        nc.vector.tensor_tensor(prod[:, u % PR], ring[:, u % RING], e_d,
                                                ALU.mult).then_inc(multiplied, 1)
                        u += 1

            dve.wait_ge(idraw_in, 16)
            nc.vector.tensor_copy(idhalf[:], idraw[:]).then_inc(idhalf_ready, 1)
            for g in range(OHG):
                split_tables(g)
            for c in range(NWC):
                split_w(c)
            dve.wait_ge(con_in, 16)
            build_hot(0)
            multiply(0)
            with dve.Fori(1, NS) as s:
                build_hot(s)
                multiply(s)

        @block.scalar
        def _(act):
            def take_group(s, g):
                if g:
                    if g >= 2:
                        act.wait_ge(stack_in[(g - 1) % 2], stacks(s, g - 1))
                    elif not is_first(s):
                        act.wait_ge(stack_in[(NG - 1) % 2], stacks(s - 1, NG - 1))
                    nc.scalar.activation(ehi[:], misc[:], ACT.Copy)
                nc.scalar.activation(eT[:, g], misc[:], ACT.Copy).then_inc(et_ready, 1)

            def load_w(s, q):
                if is_first(s):
                    act.wait_ge(w_out[q // WC], 16 * 2 * GS)
                for i in range(2):
                    act.dma_start(wst[2 * D * i:2 * D * (i + 1), q % WR].bitcast(F32), w_parts[q]).then_inc(w_in[q % WR], 16)

            def take_mlp(t, done, src):
                act.wait_ge(mlp_ready, done + t + 1)
                if t < H1 // P:
                    nc.scalar.activation(h1[:, t], src, ACT.Relu, bias=b1c[:, t:t + 1]).then_inc(mlp_ev, 1)
                elif t < NM - 1:
                    m = t - H1 // P
                    nc.scalar.activation(h2[:, m], src, ACT.Relu, bias=b2c[:, m:m + 1]).then_inc(mlp_ev, 1)
                else:
                    nc.scalar.activation(yrow[:], src[0:1], ACT.Copy).then_inc(mlp_ev, 1)

            def store_y(s):
                act.wait_ge(mlp_ev, s * NM + NM)
                act.dma_start(out[s], yrow[:]).then_inc(y_stored, 16)

            def slice_copies(s):
                if not is_first(s):
                    act.wait_ge(u_ready, s * NU)
                for q in range(WR):
                    load_w(s, q)
                n = 0
                for g in range(OHG):
                    n += kts[g]
                    act.wait_ge(hot_used, s * OHSTEPS + n)
                    take_group(s, g)
                for j in range(len(STEPS) + 1):
                    g = turn_at(j)
                    if g is not None:
                        act.wait_ge(turned, s * GG + (g - OHG + 1))
                        take_group(s, g)
                    if j in PAIRED[:NQ - WR]:
                        act.wait_ge(u_ready, s * NU + UOFF[j + 1])
                        load_w(s, PAIRED.index(j) + WR)
                    k = z_tile_done(j - 1) if j else None
                    if k is not None:
                        act.wait_ge(reduced, s * NU + UOFF[j])
                        nc.scalar.activation(zcur[:, k], zbank[:], ACT.Copy).then_inc(z_ev, 1)
                    if not is_first(s):
                        for t, k in mlp_at(j):
                            if k == MLP_K[t] - 1:
                                take_mlp(t, (s - 1) * NM, misc[:])
                                if t == NM - 1:
                                    store_y(s - 1)
                if not is_first(s):
                    act.wait_ge(y_stored, s * 16)
                act.wait_ge(z_ev, s * KT + KT)
                nc.scalar.activation(zprev[:], zcur[:], ACT.Copy).then_inc(zprev_ready, 1)

            for g in range(GG):
                act.dma_start(idx[:, g], ids_g[0, :, g]).then_inc(idx_in[g], 16)
            for g in range(OHG):
                if g >= 2:
                    act.wait_ge(part_rest, g - 1)
                for f in range(GS):
                    act.dma_start(stage(g)[:, f], tables[g * GS + f].rearrange("(p k) d -> p k d", k=kts[g]))\
                       .then_inc(table_in[g], 16)
                if g >= 1:
                    split_parts = [g - 1] if g < OHG - 1 else [g - 1, g]
                else:
                    split_parts = []
                for q in split_parts:
                    act.wait_ge(table_in[q], 16 * GS)
                    nc.scalar.activation(tsplit[q][0:PV, 0], stage(q), ACT.Copy).then_inc(part_hi, 1)
                    act.wait_ge(part_rest, q + 1)
                    nc.scalar.activation(tsplit[q][0:PV, 1], rest(q), ACT.Copy).then_inc(part_mid, 1)
            for c in range(NWC):
                act.wait_ge(wraw_in[c], 16)
                if c >= STAGES:
                    act.wait_ge(w_out[c - STAGES], 16 * 2 * GS)
                nc.scalar.activation(w_part(c, 0).bitcast(F32R), w_raw(c), ACT.Copy).then_inc(w_hi, 1)
            act.wait_ge(vec_in, 16)
            slice_copies(0)
            with act.Fori(1, NS) as s:
                slice_copies(s)
            for t in range(NM):
                take_mlp(t, (NS - 1) * NM, ring[:, t % RING, 0])
            store_y(NS - 1)
            act.wait_ge(y_stored, NS * 16)

        @block.tensor
        def _(pe):
            passed = pe_passed

            def look_up(s):
                n = 0
                for g in range(OHG):
                    if g or not is_first(s):
                        pe.wait_ge(et_ready, s * NG + g)
                    if is_first(s):
                        pe.wait_ge(part_lo, g + 1)
                    for k in range(kts[g]):
                        pe.wait_ge(hot_ready, s * OHSTEPS + n + 1)
                        for part in range(3):
                            for f in range(GS):
                                mm = nc.tensor.matmul(misc[f * D:(f + 1) * D], tsplit[g][0:PV, part, f, k],
                                                      hot[0:PV, n % OR, f], start=(k == 0 and part == 0),
                                                      stop=(k == kts[g] - 1 and part == 2))
                        mm.then_inc(hot_used, 1)
                        n += 1

            def turn(s, g):
                pe.wait_ge(gathered[g - OHG], s * (16 * NT * GS) + 16 * NT * GS)
                pe.wait_ge(et_ready, s * NG + g)
                tiles = len([t for t in range(NM) if MLP_AT[t][1] <= turn_step(g)])
                if tiles and not is_first(s):
                    pe.wait_ge(mlp_ev, (s - 1) * NM + tiles)
                for t in range(NT):
                    mm = nc.tensor.transpose(misc[:, t * P:(t + 1) * P], enat[:, g - OHG, t], ident)
                mm.then_inc(turned, 1)

            def unit_is_free(s, u, apart=False):
                if u < RING and (u or is_first(s)):
                    return
                count = s * NU + (u - RING + 1 if u else 0)
                if apart and not is_first(s):
                    wait_apart(pe, multiplied, count, passed)
                else:
                    pe.wait_ge(multiplied, count)

            def make_u(s, j):
                gs, gd = STEPS[j]
                u = UOFF[j]
                if gs != gd:
                    q = PAIRED.index(j)
                    if gd == 0:
                        pe.wait_ge(stack_in[gs % 2], stacks(s, gs))
                    pe.wait_ge(w_in[q % WR], (s * (NQ // WR) + q // WR + 1) * 32)
                    for h in range(2):
                        unit_is_free(s, u + h)
                        for i in range(2):
                            mm = nc.tensor.matmul(ring[:, (u + h) % RING, i], wst[:, q % WR, 2 * h + i],
                                                  stack[:, gs % 2, 2 * h + i], start=True, stop=True)
                        mm.then_inc(u_ready, 1)
                else:
                    if gs == 0:
                        pe.wait_ge(et_ready, s * NG + 1)
                        if is_first(s):
                            pe.wait_ge(wown_in, 16)
                    unit_is_free(s, u, apart=True)
                    for i in range(2):
                        for q in range(GS):
                            r = (q + 1 + i) % GS
                            rows = slice(r * D, (r + 1) * D)
                            mm = nc.tensor.matmul(ring[q * D:(q + 1) * D, u % RING, i], wown[rows, gs, i],
                                                  eT[rows, gs], start=True, stop=True)
                    mm.then_inc(u_ready, 1)

            def reduce(s, j):
                gs, gd = STEPS[j]
                k, m = j // SPT, j % SPT
                pick = sel[:, SELW - D - m * SLOT:SELW - m * SLOT]
                if m == 0 and (k or not is_first(s)):
                    pe.wait_ge(z_ev, s * KT + k)
                in_tile = range(k * SPT, j)
                last = z_tile_done(j) is not None
                if last and k == KT - 1:
                    if is_first(s):
                        pe.wait_ge(dense_in, 16)
                    else:
                        wait_apart(pe, dense_in, s * 16 + 16, passed)
                    for a in range(GS):
                        nc.tensor.matmul(zbank[a * D:(a + 1) * D], dsel[:, a * D:(a + 1) * D], dense[:],
                                         start=False, stop=(gs == gd and a >= 2), skip_group_check=True)
                u = UOFF[j]
                if gs != gd:
                    for h in range(2):
                        pe.wait_ge(multiplied, s * NU + u + h + 1)
                        for i in range(2):
                            a = 2 * h + i
                            fresh = m == 0 or (a >= 2 and all(STEPS[q][0] == STEPS[q][1] for q in in_tile))
                            mm = nc.tensor.matmul(zbank[a * D:(a + 1) * D], pick, prod[:, (u + h) % PR, i],
                                                  start=fresh, stop=last, skip_group_check=True)
                        mm.then_inc(reduced, 1)
                else:
                    pe.wait_ge(multiplied, s * NU + u + 1)
                    for i, rows in enumerate((P, 2 * D)):
                        mm = nc.tensor.matmul(zbank[i * D:(i + 1) * D], pick[0:rows], prod[0:rows, u % PR, i],
                                              start=(m == 0), stop=last, skip_group_check=True)
                    mm.then_inc(reduced, 1)

            def mlp(s, t, k, dst):
                if t < H1 // P:
                    if t == 0 and k == 0:
                        pe.wait_ge(zprev_ready, s + 1)
                    w, x = w1s[:, k, t * P:(t + 1) * P], zprev[:, k]
                elif t < NM - 1:
                    if k == 0:
                        pe.wait_ge(mlp_ev, s * NM + H1 // P)
                    m = t - H1 // P
                    w, x = w2s[:, k, m * P:(m + 1) * P], h1[:, k]
                else:
                    if k == 0:
                        pe.wait_ge(mlp_ev, s * NM + NM - 1)
                    w, x, dst = w3c[:, k:k + 1], h2[:, k], dst[0:1]
                mm = nc.tensor.matmul(dst, w, x, start=(k == 0), stop=(k == MLP_K[t] - 1))
                if k == MLP_K[t] - 1:
                    mm.then_inc(mlp_ready, 1)

            def slice_steps(s):
                look_up(s)
                make_u(s, 0)
                held_by_group = True
                groups = OHG
                for j in range(len(STEPS)):
                    g = turn_at(j)
                    if g is not None:
                        turn(s, g)
                        held_by_group, groups = True, g + 1
                    if j + 1 < len(STEPS):
                        make_u(s, j + 1)
                    if j:
                        reduce(s, j - 1)
                    if not is_first(s):
                        for t, k in mlp_at(j):
                            if k == 0 and held_by_group:
                                pe.wait_ge(et_ready, s * NG + groups)
                            elif k == 0:
                                pe.wait_ge(mlp_ev, (s - 1) * NM + t)
                            held_by_group = False
                            mlp(s - 1, t, k, misc[:])
                reduce(s, len(STEPS) - 1)
                if not is_first(s):
                    pe.wait_ge(mlp_ev, s * NM)

            pe.wait_ge(con_in, 16)
            slice_steps(0)
            pe.wait_ge(w1_in, 16)
            pe.wait_ge(w2_in, 16)
            pe.wait_ge(vec_in, 16)
            with pe.Fori(1, NS) as s:
                slice_steps(s)
            for t in range(NM):
                if t == 0:
                    pe.wait_ge(multiplied, NS * NU)
                if t >= RING:
                    pe.wait_ge(mlp_ev, (NS - 1) * NM + t - RING + 1)
                for k in range(MLP_K[t]):
                    mlp(NS - 1, t, k, ring[:, t % RING, 0])


def field_order(vocab):
    small = sorted((f for f in range(F) if vocab[f] % PV == 0), key=lambda f: (vocab[f], f))[:OHG * GS]
    return small + [f for f in range(F) if f not in small]


def pair_index(i, j):
    return i * (2 * F - i - 1) // 2 + (j - i - 1)


def lay_out_pairs(W, order):
    def mat(src, dst):
        return W[pair_index(src, dst)] if src < dst else W[pair_index(dst, src)].T

    pairs = np.empty((GS, D, NQ, GS, D), W.dtype)
    own = np.empty((GS, D, NG, 2, D), W.dtype)
    for a in range(GS):
        for q, j in enumerate(PAIRED):
            gs, gd = STEPS[j]
            for b in range(GS):
                pairs[a, :, q, b] = mat(order[gs * GS + a], order[gd * GS + b])
        for g in range(NG):
            for i in range(2):
                own[a, :, g, i] = mat(order[g * GS + a], order[g * GS + (a - 1 - i) % GS])
    return pairs.reshape(P, NQ * P), own.reshape(P, NG, 2, D)


def top_rows(order):
    rows = np.zeros((P, KT), np.int64)
    for j, (gs, gd) in enumerate(STEPS):
        k, m = j // SPT, j % SPT
        for a in range(GS):
            for q in range(GS):
                if gs != gd:
                    pair = (order[gs * GS + a], order[gd * GS + q])
                elif a == 0 or (a == 1 and q < 2):
                    pair = (order[gs * GS + (q + 1 + a) % GS], order[gs * GS + q])
                else:
                    continue
                rows[a * D + m * SLOT + q, k] = pair_index(min(pair), max(pair))
    for a in range(GS):
        for r in range(SLOT):
            rows[a * D + (SPT - 1) * SLOT + r, KT - 1] = F * (F - 1) // 2 + a * SLOT + r
    return rows


def constants(kts):
    KTM = max(kts)
    sel = np.zeros((P, SELW), np.float32)
    sel[np.arange(P), SELW - D + np.arange(P) // D] = 1
    dsel = np.zeros((P, GS * D), np.float32)
    for r in range(DENSE):
        dsel[r, (r // SLOT) * D + (SPT - 1) * SLOT + r % SLOT] = 1
    vcol = np.zeros((P, len(kts), KTM), np.float32)
    for g, k in enumerate(kts):
        vcol[:, g, :k] = np.arange(P)[:, None] * k + np.arange(k)
    return np.concatenate([sel, dsel, vcol.reshape(P, -1), np.eye(P, dtype=np.float32)], axis=1)


def kernel(dense_ctx, ids, W_top1, b_top1, W_top2, b_top2, W_top3, L0_rec_W, **tables):
    import numpy as _np
    import concourse.bacc as _bacc
    from concourse import mybir as _mybir
    from concourse.bass_utils import run_bass_kernel_spmd as _run

    tabs = [_np.asarray(tables[f"tbl_{f}"]) for f in range(F)]
    order = field_order([t.shape[0] for t in tabs])
    vocab = [tabs[f].shape[0] for f in order]
    kts = [vocab[g * GS] // PV for g in range(OHG)]
    idT = _np.asarray(ids).T[order]
    noh = OHG * GS
    w_pairs, w_own = lay_out_pairs(_np.asarray(L0_rec_W), order)
    arrays = {
        "ids_oh": idT[:noh].reshape(P, -1),
        "ids_g": idT[noh:].reshape(GG, GS, NS, NT, P).transpose(2, 4, 0, 3, 1),
        "ctxT": _np.asarray(dense_ctx).reshape(NS, N, DENSE).transpose(0, 2, 1),
        "w_pairs": w_pairs,
        "w_own": w_own,
        "w1": _np.asarray(W_top1)[top_rows(order)],
        "w2": _np.asarray(W_top2).reshape(H1 // P, P, H2).transpose(1, 0, 2),
        "vecs": _np.concatenate([_np.asarray(x).reshape(-1, P).T for x in (b_top1, b_top2, W_top3)], axis=1),
        "consts": constants(kts),
    }
    for i, f in enumerate(order):
        arrays[f"table{i}"] = tabs[f]
    arrays = {k: _np.ascontiguousarray(v) for k, v in arrays.items()}

    nc = _bacc.Bacc("TRN2", target_bir_lowering=False, num_devices=1)
    ap = {k: nc.dram_tensor(k, v.shape, _mybir.dt.from_np(v.dtype), kind="ExternalInput").ap()
          for k, v in arrays.items()}
    scratch = nc.dram_tensor("scratch", (noh * B,), F16, kind="Internal").ap()
    w_parts = nc.dram_tensor("w_parts", (NQ, 2 * D, GS, P), F32, kind="Internal").ap()
    out = nc.dram_tensor("y", (NS, 1, N), F32, kind="ExternalOutput").ap()
    build(nc, vocab, ap["ids_oh"], ap["ids_g"], ap["ctxT"], ap["w_pairs"], ap["w_own"], ap["w1"], ap["w2"], ap["vecs"],
          ap["consts"], [ap[f"table{i}"] for i in range(F)], scratch, w_parts, out)
    r = _run(nc, [arrays], core_ids=[0])
    return r.results[0]["y"].reshape(B, 1)
```

```python
from contextlib import ExitStack

import numpy as np

import concourse.bass as bass
from concourse import mybir

P = 128
B = 2048
F = 40
D = 32
NS = 4
N = B // NS
NT = N // P
GS = P // D
NG = F // GS
OHG = 2
GG = NG - OHG
PV = 125
SLOT = 4
SPT = D // SLOT
STEPS = [(gs, gd) for gs in range(NG) for gd in range(gs + 1)]
ROW = [g * (g + 1) // 2 for g in range(NG + 1)]
OWN = [(3, 0, 0), (0, 1, 0), (0, 2, 0), (2, 3, 0), (1, 2, 1), (1, 3, 1)]
NJ = len(STEPS)
KT = (NJ + SPT - 1) // SPT
UNITS = [2 if gs != gd else 1 for gs, gd in STEPS]
UOFF = [sum(UNITS[:j]) for j in range(NJ + 1)]
NU = UOFF[-1]
LAST = NJ - 1
H1, H2 = 512, 256
RING = 3
PR = 4
WR = 5
WC = 4
NWC = (NJ + WC - 1) // WC
STAGES = 3
SR = 4
ZC = 3
OR = 5
DENSE = 16
SELW = D + (SPT - 1) * SLOT
ALU = mybir.AluOpType
ACT = mybir.ActivationFunctionType
F32, F32R, BF16, F16, I32 = (mybir.dt.float32, mybir.dt.float32r, mybir.dt.bfloat16, mybir.dt.float16,
                             mybir.dt.int32)

EARLY = 3
TURN_AT = {3: 0, 4: 2, 5: 8, 6: 16, 7: 22, 8: 28, 9: 32}
EARLY_TURN_AT = {2: 50}
LOOKUP_AT = [(33, 41), (44, 49)]
MOVE_AT = {0: 47, 1: 50}
HOT_LEAD = 2
FIRST_TURN_AT = {3: 0, 4: 5, 5: 10, 6: 16, 7: 24, 8: 30, 9: 38}
FIRST_LOOKUP_AT = [(30, 37), (39, 46)]
SPLIT_AT = {c: 8 + 2 * (c - KT) for c in range(KT, NWC)}
MLP_AT = [(3, 8), (9, 16), (17, 22), (23, 28), (29, 32), (41, 43), (43, 44)]
MLP_K = [KT] * (H1 // P) + [H1 // P] * (H2 // P) + [H2 // P]
NM = len(MLP_K)
W1_AT = 42
ZCOPY_AT = 29


def is_first(s):
    return isinstance(s, int) and s == 0


def turn_at(s, j):
    table = FIRST_TURN_AT if is_first(s) else TURN_AT
    return next((g for g in table if table[g] == j), None)


def early_turn_at(j):
    return next((g for g in EARLY_TURN_AT if EARLY_TURN_AT[g] == j), None)


def lookups_at(s, j, kts):
    spread = FIRST_LOOKUP_AT if is_first(s) else LOOKUP_AT
    return [(g, k) for g, (a, b) in enumerate(spread) for k in range(kts[g]) if a + k * (b - a) // kts[g] == j]


def take_at(s, j):
    spread = FIRST_LOOKUP_AT if is_first(s) else LOOKUP_AT
    return next((g for g, (a, b) in enumerate(spread) if b - 1 == j), None)


def nth(s, g):
    steps = [(step, 0, group) for group, step in FIRST_TURN_AT.items()]
    steps += [(step, 1, group) for group, step in EARLY_TURN_AT.items()]
    steps += [(b - 1, 1, group) for group, (a, b) in enumerate(FIRST_LOOKUP_AT)]
    order = [(slice_, group) for _, slice_, group in sorted(steps)]
    return EARLY + order.index((s, g)) if isinstance(s, int) and (s, g) in order else s * NG + g


def mlp_at(j):
    return [(t, k) for t, (a, b) in enumerate(MLP_AT) for k in range(MLP_K[t])
            if a + k * (b - a) // MLP_K[t] == j]


def ring_slot(u):
    return 1 if u == NU - 1 else u % RING


def unit_before(u):
    return next(v for v in range(u - 1, -NU, -1) if ring_slot(v % NU) == ring_slot(u))


def stack_slot(g):
    return (g - 1) % (SR - 1) if g else SR - 1


def row_before(g):
    return next((back, r) for back, rows in ((0, range(g - 1, -1, -1)), (1, range(NG - 1, -1, -1)))
                for r in rows if stack_slot(r) == stack_slot(g))


def z_tile_done(j):
    return j // SPT if j % SPT == SPT - 1 or j == NJ - 1 else None


def build(nc, vocab, ids_oh, ids_g, ctxT, w_pairs, w1, w2, vecs, consts, tables, scratch,
          w_parts, out):
    kts = [vocab[g * GS] // PV for g in range(OHG)]
    KTM = max(kts)
    OHSTEPS = sum(kts)
    assert all(v == kts[i // GS] * PV for i, v in enumerate(vocab[:OHG * GS]))

    with ExitStack() as ctx:
        def sb(name, shape, dt):
            return ctx.enter_context(nc.sbuf_tensor(name, shape, dt))

        def sem(name):
            return ctx.enter_context(nc.semaphore(name))

        ring = ctx.enter_context(nc.psum_tensor("ring", [P, RING, 2, N], F32))
        zbank = ctx.enter_context(nc.psum_tensor("zbank", [P, N], F32))
        misc = ctx.enter_context(nc.psum_tensor("misc", [P, N], F32))

        wst = sb("wst", [P, WR, GS, P], F32R)
        stack = sb("stack", [P, SR, GS, N], F32R)
        ehi = sb("ehi", [P, N], F32R)
        elo = sb("elo", [P, N], F32R)
        w1s = sb("w1s", [P, KT, H1], F32)
        w2s = sb("w2s", [P, H1 // P, H2], F32)
        vec = sb("vec", [P, 8], F32)
        con = sb("con", [P, consts.shape[1]], F32)
        enat = sb("enat", [P, GG, NT, P], F32)
        eT = sb("eT", [P, NG, N], F32)
        enext = sb("enext", [P, OHG, N], F32)
        idx = sb("idx", [P, GG, NT, GS], I32)
        idraw = sb("idraw", [P, OHG * GS * B // P], I32)
        idhalf = sb("idhalf", [P, OHG * GS * B // P], F16)
        idb = sb("idb", [P, OHG, GS, N], F16)
        hot = sb("hot", [P, OR, GS, N], BF16)
        tsplit = [sb(f"tsplit{g}", [P, 3, GS, kts[g], D], BF16) for g in range(OHG)]
        prod = sb("prod", [P, PR, 2, N], F32)
        zcur = sb("zcur", [P, ZC, N], F32)
        zprev = sb("zprev", [P, KT, N], F32)
        h1 = sb("h1", [P, H1 // P, N], F32)
        h2 = sb("h2", [P, H2 // P, N], F32)
        yrow = sb("yrow", [1, N], F32)
        dense = sb("dense", [DENSE, N], F32)

        def taken_to(g):
            return enext[:, g] if g < OHG else eT[:, g]

        def stage(g):
            return h1[:].rearrange("p k n -> p (k n)")[0:PV, (g % 2) * GS * KTM * D:(g % 2 + 1) * GS * KTM * D]\
                .rearrange("p (f k d) -> p f k d", f=GS, d=D)

        def rest(g):
            return h2[:].rearrange("p k n -> p (k n)")[0:PV, 0:GS * KTM * D].rearrange("p (f k d) -> p f k d", f=GS, d=D)

        def w_raw(c):
            return w1s[0:w_rows(c), c % KT]

        def w_part(c, part):
            return prod[0:w_rows(c), c, part] if c < PR else zprev[0:w_rows(c), part * STAGES + (c - PR) % STAGES]

        def w_rows(c):
            return min(WC, NJ - c * WC) * D

        sel = con[:, 0:SELW]
        dsel = con[0:DENSE, SELW:SELW + GS * D]
        c0 = SELW + GS * D
        vcol = [con[:, c0 + g * KTM:c0 + (g + 1) * KTM] for g in range(OHG)]
        ident = con[:, c0 + OHG * KTM:c0 + OHG * KTM + P]
        b1c, b2c, w3c = vec[:, 0:4], vec[:, 4:6], vec[:, 6:8]

        idraw_in = sem("idraw_in")
        idhalf_ready = sem("idhalf_ready")
        idhalf_out = sem("idhalf_out")
        con_in = sem("con_in")
        vec_in = sem("vec_in")
        wraw_in = [sem(f"wraw_in{c}") for c in range(NWC)]
        w_hi = sem("w_hi")
        w_lo = sem("w_lo")
        w_out = [sem(f"w_out{c}") for c in range(NWC)]
        w_in = [sem(f"w_in{i}") for i in range(WR)]
        elo_ready = sem("elo_ready")
        elo_stacked = sem("elo_stacked")
        stack_in = [sem(f"stack_in{i}") for i in range(SR)]
        w1_in = sem("w1_in")
        w2_in = sem("w2_in")
        table_in = [sem(f"table_in{g}") for g in range(OHG)]
        part_hi = sem("part_hi")
        part_rest = sem("part_rest")
        part_mid = sem("part_mid")
        part_lo = sem("part_lo")
        idb_in = [sem(f"idb_in{g}") for g in range(OHG)]
        idx_in = [sem(f"idx_in{g}") for g in range(GG)]
        gathered = [sem(f"gathered{g}") for g in range(GG)]
        dense_in = sem("dense_in")
        hot_ready = sem("hot_ready")
        hot_used = sem("hot_used")
        turned = sem("turned")
        mlp_ready = sem("mlp_ready")
        et_ready = sem("et_ready")
        et_moved = sem("et_moved")
        ehi_stacked = sem("ehi_stacked")
        mlp_ev = sem("mlp_ev")
        u_ready = sem("u_ready")
        multiplied = sem("multiplied")
        reduced = sem("reduced")
        z_ev = sem("z_ev")
        z_moved = sem("z_moved")
        y_stored = sem("y_stored")
        pool_passed = sem("pool_passed")
        pe_passed = sem("pe_passed")

        def last_dst(t):
            return ring[:, t % RING, 0] if t else misc[:]

        block = ctx.enter_context(nc.Block())

        def stacks(s, g):
            per_slice = sum(stack_slot(r) == stack_slot(g) for r in range(NG))
            return 32 * (s * per_slice + sum(stack_slot(r) == stack_slot(g) for r in range(g + 1)))

        def wait_apart(eng, s, value, passed):
            eng.wait_ge(s, value)
            eng.sem_inc(passed, 1)

        @block.sync
        def _(sp):
            def load_raw(c):
                sp.dma_start(w_raw(c), w_pairs[c * WC * D:c * WC * D + w_rows(c)]).then_inc(wraw_in[c], 16)

            def load_ids_broadcast(s):
                for g in range(OHG):
                    src = scratch.rearrange("(g f s n) -> s g f n", g=OHG, f=GS, s=NS)[s, g]
                    sp.dma_start(idb[:, g], src.partition_broadcast(P)).then_inc(idb_in[g], 16)

            def load_indices(s, g):
                sp.wait_ge(gathered[g - OHG], s * (16 * NT * GS))
                sp.dma_start(idx[:, g - OHG], ids_g[s, :, g - OHG]).then_inc(idx_in[g - OHG], 16)

            def build_stack(s, g):
                slot = stack_slot(g)
                sp.wait_ge(ehi_stacked, nth(s, g) + 1)
                sp.dma_start(stack[D:2 * D, slot].bitcast(F32), stack[0:D, slot].bitcast(F32)).then_inc(stack_in[slot], 16)
                sp.wait_ge(elo_stacked, nth(s, g) + 1)
                sp.dma_start(stack[3 * D:4 * D, slot].bitcast(F32), stack[2 * D:3 * D, slot].bitcast(F32)).then_inc(stack_in[slot], 16)

            def slice_loads(s, last=False):
                if not last:
                    sp.wait_ge(hot_ready, s * OHSTEPS + OHSTEPS)
                    load_ids_broadcast(s + 1)
                    load_indices(s + 1, OHG)
                if not is_first(s):
                    sp.wait_ge(reduced, s * NU)
                    sp.dma_start(dense[:], ctxT[s]).then_inc(dense_in, 16)
                for j in range(NJ):
                    if is_first(s):
                        for c in SPLIT_AT:
                            if SPLIT_AT[c] == j:
                                store_parts(c)
                    g = turn_at(s, j)
                    if g is not None:
                        build_stack(s, g)
                        if not last:
                            load_indices(s + 1, g)
                    g = early_turn_at(j)
                    if g is not None and not last:
                        build_stack(s + 1, g)
                    g = take_at(s, j)
                    if g is not None and not last:
                        build_stack(s + 1, g)
                    if is_first(s) and j == W1_AT:
                        sp.wait_ge(w_lo, NWC)
                        sp.dma_start(w1s[:], w1).then_inc(w1_in, 16)
                        sp.dma_start(w2s[:], w2).then_inc(w2_in, 16)

            def store_parts(c):
                sp.wait_ge(w_lo, c + 1)
                for part in range(2):
                    n = w_rows(c) // D
                    sp.dma_start(w_parts[c * WC:c * WC + n, part], w_part(c, part)).then_inc(w_out[c], 16)
                if c + KT < NWC:
                    load_raw(c + KT)

            sp.dma_start(idraw[:], ids_oh).then_inc(idraw_in, 16)
            load_raw(0)
            load_raw(1)
            sp.wait_ge(idhalf_ready, 1)
            sp.dma_start(scratch.rearrange("(p n) -> p n", p=P), idhalf[:]).then_inc(idhalf_out, 16)
            sp.dma_start(idx[:, 0], ids_g[0, :, 0]).then_inc(idx_in[0], 16)
            sp.dma_start(con[:], consts).then_inc(con_in, 16)
            load_raw(2)
            load_raw(3)
            sp.wait_ge(idhalf_out, 16)
            load_ids_broadcast(0)
            for c in range(4, KT):
                load_raw(c)
            for c in range(PR):
                store_parts(c)
            build_stack(0, 0)
            for c in range(PR, KT):
                store_parts(c)
            build_stack(0, 1)
            sp.dma_start(dense[:], ctxT[0]).then_inc(dense_in, 16)
            build_stack(0, 2)
            sp.dma_start(vec[:], vecs).then_inc(vec_in, 16)

            slice_loads(0)
            with sp.Fori(1, NS - 1) as s:
                slice_loads(s)
            slice_loads(NS - 1, last=True)

        @block.gpsimd
        def _(pool):
            def gather_slice(s):
                for g in range(GG):
                    pool.wait_ge(idx_in[g], s * 16 + 16)
                    if not is_first(s):
                        wait_apart(pool, turned, (s - 1) * GG + g + 1, pool_passed)
                    for f in range(GS):
                        for t in range(NT):
                            pool.indirect_dma_start(
                                out=enat[:, g, t, f * D:(f + 1) * D], out_offset=None,
                                in_=tables[(OHG + g) * GS + f],
                                in_offset=bass.IndirectOffsetOnAxis(ap=idx[:, g, t, f:f + 1], axis=0),
                            ).then_inc(gathered[g], 16)

            gather_slice(0)
            with pool.Fori(1, NS) as s:
                gather_slice(s)

        @block.vector
        def _(dve):
            def rest_of_tables(g):
                dve.wait_ge(part_hi, g + 1)
                if g:
                    dve.wait_ge(part_lo, g)
                nc.vector.tensor_tensor(rest(g), stage(g), tsplit[g][0:PV, 0], ALU.subtract).then_inc(part_rest, 1)

            def low_tables(g):
                dve.wait_ge(part_mid, g + 1)
                nc.vector.tensor_tensor(tsplit[g][0:PV, 2], rest(g), tsplit[g][0:PV, 1],
                                        ALU.subtract).then_inc(part_lo, 1)

            def build_hot(s, g, k):
                n = sum(kts[:g]) + k
                if k == 0:
                    dve.wait_ge(idb_in[g], s * 16 + 16)
                if n >= OR:
                    dve.wait_ge(hot_used, s * OHSTEPS + (n - OR + 1))
                elif n == 0 and not is_first(s):
                    dve.wait_ge(hot_used, s * OHSTEPS)
                nc.vector.tensor_scalar(hot[0:PV, n % OR], idb[0:PV, g], vcol[g][0:PV, k:k + 1],
                                        None, ALU.is_equal).then_inc(hot_ready, 1)

            def split_w(c):
                dve.wait_ge(w_hi, c + 1)
                if c >= PR + STAGES:
                    dve.wait_ge(w_out[c - STAGES], 16 * 2)
                nc.vector.tensor_tensor(w_part(c, 1).bitcast(F32R), w_raw(c), w_part(c, 0),
                                        ALU.subtract).then_inc(w_lo, 1)

            def low_parts(s, g):
                dve.wait_ge(et_ready, nth(s, g) + 1)
                if g or not is_first(s):
                    dve.wait_ge(elo_stacked, nth(s, g))
                nc.vector.tensor_tensor(elo[:], taken_to(g), ehi[:].bitcast(F32),
                                        ALU.subtract).then_inc(elo_ready, 1)

            def multiply(s, last=False):
                for j, (gs, gd) in enumerate(STEPS):
                    if not last:
                        for g, k in lookups_at(s, j + HOT_LEAD, kts):
                            build_hot(s + 1, g, k)
                    for u in range(UOFF[j], UOFF[j + 1]):
                        dve.wait_ge(u_ready, s * NU + u + 1)
                        if j in (0, 2):
                            dve.wait_ge(et_moved, s * OHG + gd + 1)
                        if u >= PR or not is_first(s):
                            dve.wait_ge(reduced, s * NU + (u - PR + 1))
                        elif u < PR:
                            dve.wait_ge(w_out[u], 16 * 2)
                        e_d = eT[:, gd:gd + 1, :].to_broadcast([P, 2, N])
                        nc.vector.tensor_tensor(prod[:, u % PR], ring[:, ring_slot(u)], e_d,
                                                ALU.mult).then_inc(multiplied, 1)
                    g = turn_at(s, j - 1)
                    if g is not None:
                        low_parts(s, g)
                    if not last:
                        for g in (early_turn_at(j - 1), take_at(s, j - 1)):
                            if g is not None:
                                low_parts(s + 1, g)
                    if is_first(s):
                        for c in SPLIT_AT:
                            if SPLIT_AT[c] == j:
                                split_w(c)

            dve.wait_ge(idraw_in, 16)
            nc.vector.tensor_copy(idhalf[:], idraw[:]).then_inc(idhalf_ready, 1)
            split_w(0)
            rest_of_tables(0)
            split_w(1)
            low_tables(0)
            dve.wait_ge(con_in, 16)
            for k in range(kts[0]):
                if k == OR:
                    rest_of_tables(1)
                elif k == OR + 2:
                    low_tables(1)
                build_hot(0, 0, k)
            split_w(2)
            split_w(3)
            for k in range(kts[1]):
                build_hot(0, 1, k)
                if k == OR - 1:
                    low_parts(0, 0)
            for c in range(PR, KT):
                split_w(c)
            low_parts(0, 1)
            low_parts(0, 2)
            multiply(0)
            with dve.Fori(1, NS - 1) as s:
                multiply(s)
            multiply(NS - 1, last=True)

        @block.scalar
        def _(act):
            def take_group(s, g, src=misc):
                if g >= OHG and not is_first(s):
                    act.wait_ge(multiplied, (s - 1) * NU + UOFF[ROW[NG - 1] + g + 1])
                nc.scalar.activation(ehi[:], src[:], ACT.Copy)
                nc.scalar.activation(taken_to(g), src[:], ACT.Copy).then_inc(et_ready, 1)
                back, row = row_before(g)
                if not (back and is_first(s)):
                    act.wait_ge(u_ready, (s - back) * NU + UOFF[ROW[row + 1]])
                act.wait_ge(et_ready, nth(s, g) + 1)
                for f in range(GS):
                    cp = nc.scalar.activation(stack[0:D, stack_slot(g), f], taken_to(g)[f * D:(f + 1) * D], ACT.Copy)
                cp.then_inc(ehi_stacked, 1)
                act.wait_ge(elo_ready, nth(s, g) + 1)
                for f in range(GS):
                    cp = nc.scalar.activation(stack[2 * D:3 * D, stack_slot(g), f], elo[f * D:(f + 1) * D].bitcast(F32), ACT.Copy)
                cp.then_inc(elo_stacked, 1)

            def move_group(s, g):
                if not is_first(s):
                    act.wait_ge(multiplied, (s - 1) * NU + UOFF[ROW[NG - 1] + g + 1])
                nc.scalar.activation(eT[:, g], enext[:, g], ACT.Copy).then_inc(et_moved, 1)

            def load_w(s, j):
                if is_first(s):
                    act.wait_ge(w_out[j // WC], 16 * 2)
                act.dma_start(wst[:, j % WR].bitcast(F32), w_parts[j].partition_broadcast(2)).then_inc(w_in[j % WR], 16)

            def split_w(c):
                act.wait_ge(wraw_in[c], 16)
                if c >= PR + STAGES:
                    act.wait_ge(w_out[c - STAGES], 16 * 2)
                nc.scalar.activation(w_part(c, 0).bitcast(F32R), w_raw(c), ACT.Copy).then_inc(w_hi, 1)

            def take_z(s, k):
                dst = zcur[:, k] if k < ZC else zprev[:, k]
                nc.scalar.activation(dst, zbank[:], ACT.Copy).then_inc(z_ev, 1)

            def take_mlp(t, done, src):
                act.wait_ge(mlp_ready, done + t + 1)
                if t < H1 // P:
                    nc.scalar.activation(h1[:, t], src, ACT.Relu, bias=b1c[:, t:t + 1]).then_inc(mlp_ev, 1)
                elif t < NM - 1:
                    m = t - H1 // P
                    nc.scalar.activation(h2[:, m], src, ACT.Relu, bias=b2c[:, m:m + 1]).then_inc(mlp_ev, 1)
                else:
                    nc.scalar.activation(yrow[:], src[0:1], ACT.Copy).then_inc(mlp_ev, 1)

            def store_y(s):
                act.wait_ge(mlp_ev, s * NM + NM)
                act.dma_start(out[s], yrow[:]).then_inc(y_stored, 16)

            def slice_copies(s, last=False):
                if not is_first(s):
                    act.wait_ge(reduced, s * NU)
                    take_z(s - 1, KT - 1)
                for j in range(NJ):
                    if is_first(s):
                        for c in SPLIT_AT:
                            if SPLIT_AT[c] == j:
                                split_w(c)
                    if j + WR < NJ or not last:
                        act.wait_ge(u_ready, s * NU + UOFF[j + 1])
                        load_w(s + (j + WR) // NJ, (j + WR) % NJ)
                    k = z_tile_done(j - 1) if j else None
                    if k is not None:
                        act.wait_ge(reduced, s * NU + UOFF[j])
                        take_z(s, k)
                    g = turn_at(s, j)
                    if g is not None:
                        act.wait_ge(turned, s * GG + (g - OHG + 1))
                        take_group(s, g)
                    g = early_turn_at(j)
                    if g is not None and not last:
                        act.wait_ge(turned, (s + 1) * GG + (g - OHG + 1))
                        take_group(s + 1, g)
                    if not is_first(s):
                        for t, k in mlp_at(j):
                            if k == MLP_K[t] - 1:
                                take_mlp(t, (s - 1) * NM, misc[:])
                                if t == NM - 1:
                                    store_y(s - 1)
                    if j == ZCOPY_AT:
                        if is_first(s):
                            for c in range(NWC - STAGES, NWC):
                                act.wait_ge(w_out[c], 16 * 2)
                        act.wait_ge(z_ev, s * KT + ZC)
                        nc.scalar.activation(zprev[:, 0:ZC], zcur[:], ACT.Copy).then_inc(z_moved, 1)
                    g = take_at(s, j)
                    if g is not None and not last:
                        act.wait_ge(hot_used, (s + 1) * OHSTEPS + sum(kts[:g + 1]))
                        take_group(s + 1, g)
                    for g in MOVE_AT:
                        if MOVE_AT[g] == j and not last:
                            move_group(s + 1, g)
                if not is_first(s):
                    act.wait_ge(y_stored, s * 16)

            def load_tables(g):
                for f in range(GS):
                    act.dma_start(stage(g)[:, f], tables[g * GS + f].rearrange("(p k) d -> p k d", k=kts[g]))\
                       .then_inc(table_in[g], 16)

            def split_tables(g):
                act.wait_ge(table_in[g], 16 * GS)
                nc.scalar.activation(tsplit[g][0:PV, 0], stage(g), ACT.Copy).then_inc(part_hi, 1)
                act.wait_ge(part_rest, g + 1)
                nc.scalar.activation(tsplit[g][0:PV, 1], rest(g), ACT.Copy).then_inc(part_mid, 1)

            load_tables(0)
            split_w(0)
            split_w(1)
            load_tables(1)
            split_tables(0)
            split_tables(1)
            for g in range(1, GG):
                act.dma_start(idx[:, g], ids_g[0, :, g]).then_inc(idx_in[g], 16)
            for c in range(2, KT):
                split_w(c)
            for j in range(WR):
                load_w(0, j)
            for g in range(OHG):
                act.wait_ge(hot_used, sum(kts[:g + 1]))
                take_group(0, g, zbank if g else misc)
                move_group(0, g)
            act.wait_ge(turned, 1)
            take_group(0, 2)
            slice_copies(0)
            act.wait_ge(vec_in, 16)
            with act.Fori(1, NS - 1) as s:
                slice_copies(s)
            slice_copies(NS - 1, last=True)
            act.wait_ge(reduced, NS * NU)
            take_z(NS - 1, KT - 1)
            for t in range(NM):
                take_mlp(t, (NS - 1) * NM, last_dst(t))
            store_y(NS - 1)
            act.wait_ge(y_stored, NS * 16)

        @block.tensor
        def _(pe):
            def look_up(s, g, k, dst=misc):
                n = sum(kts[:g]) + k
                if k == 0 and is_first(s):
                    pe.wait_ge(part_lo, g + 1)
                pe.wait_ge(hot_ready, s * OHSTEPS + n + 1)
                for part in range(3):
                    for f in range(GS):
                        mm = nc.tensor.matmul(dst[f * D:(f + 1) * D], tsplit[g][0:PV, part, f, k],
                                              hot[0:PV, n % OR, f], start=(k == 0 and part == 0),
                                              stop=(k == kts[g] - 1 and part == 2))
                mm.then_inc(hot_used, 1)

            def turn(s, g):
                pe.wait_ge(gathered[g - OHG], s * (16 * NT * GS) + 16 * NT * GS)
                for t in range(NT):
                    mm = nc.tensor.transpose(misc[:, t * P:(t + 1) * P], enat[:, g - OHG, t], ident)
                mm.then_inc(turned, 1)

            def make_unit(s, u):
                j = next(i for i in range(NJ) if UOFF[i + 1] > u)
                gs, gd = STEPS[j]
                h = u - UOFF[j]
                if h == 0:
                    if gd == 0:
                        pe.wait_ge(stack_in[stack_slot(gs)], stacks(s, gs))
                    pe.wait_ge(w_in[j % WR], (s * (NJ // WR) + j // WR + 1) * 16)
                v = unit_before(u)
                if v >= 0 or not is_first(s):
                    pe.wait_ge(multiplied, s * NU + v + 1)
                if gs != gd:
                    parts = [(2 * h + i, i) for i in range(2)]
                else:
                    parts = [(a, i) for i in range(2) for a in sorted({a for a, d, half in OWN if half == i})]
                for n, (a, i) in enumerate(parts):
                    mm = nc.tensor.matmul(ring[:, ring_slot(u), i], wst[:, j % WR, a], stack[:, stack_slot(gs), a],
                                          start=(n == 0 or parts[n - 1][1] != i),
                                          stop=(n == len(parts) - 1 or parts[n + 1][1] != i))
                mm.then_inc(u_ready, 1)

            def reduce(s, j):
                gs, gd = STEPS[j]
                k, m = j // SPT, j % SPT
                pick = sel[:, SELW - D - m * SLOT:SELW - m * SLOT]
                if m == 0 and (k or not is_first(s)):
                    pe.wait_ge(z_ev, s * KT + k)
                in_tile = range(k * SPT, j)
                last = z_tile_done(j) is not None
                if last and k == KT - 1:
                    if is_first(s):
                        pe.wait_ge(dense_in, 16)
                    else:
                        wait_apart(pe, dense_in, s * 16 + 16, pe_passed)
                    for a in range(GS):
                        nc.tensor.matmul(zbank[a * D:(a + 1) * D], dsel[:, a * D:(a + 1) * D], dense[:],
                                         start=False, stop=(gs == gd and a >= 2), skip_group_check=True)
                u = UOFF[j]
                if gs != gd:
                    for h in range(2):
                        pe.wait_ge(multiplied, s * NU + u + h + 1)
                        for i in range(2):
                            a = 2 * h + i
                            fresh = m == 0 or (a >= 2 and all(STEPS[q][0] == STEPS[q][1] for q in in_tile))
                            mm = nc.tensor.matmul(zbank[a * D:(a + 1) * D], pick, prod[:, (u + h) % PR, i],
                                                  start=fresh, stop=last, skip_group_check=True)
                        mm.then_inc(reduced, 1)
                else:
                    pe.wait_ge(multiplied, s * NU + u + 1)
                    for i in range(2):
                        mm = nc.tensor.matmul(zbank[i * D:(i + 1) * D], pick, prod[:, u % PR, i],
                                              start=(m == 0), stop=last, skip_group_check=True)
                    mm.then_inc(reduced, 1)

            def mlp(s, t, k, dst):
                if t < H1 // P:
                    if t == 0 and k == 0:
                        pe.wait_ge(z_moved, s + 1)
                    if t == 0 and k >= ZC:
                        pe.wait_ge(z_ev, s * KT + k + 1)
                    w, x = w1s[:, k, t * P:(t + 1) * P], zprev[:, k]
                elif t < NM - 1:
                    if k == 0:
                        pe.wait_ge(mlp_ev, s * NM + H1 // P)
                    m = t - H1 // P
                    w, x = w2s[:, k, m * P:(m + 1) * P], h1[:, k]
                else:
                    if k == 0:
                        pe.wait_ge(mlp_ev, s * NM + NM - 1)
                    w, x, dst = w3c[:, k:k + 1], h2[:, k], dst[0:1]
                mm = nc.tensor.matmul(dst, w, x, start=(k == 0), stop=(k == MLP_K[t] - 1))
                if k == MLP_K[t] - 1:
                    mm.then_inc(mlp_ready, 1)

            def slice_steps(s, last=False):
                misc_free = (et_ready, s * NG + EARLY)
                for j in range(NJ):
                    if j < LAST:
                        make_unit(s, UOFF[j + 1])
                    elif not last:
                        make_unit(s + 1, 0)
                    if j:
                        reduce(s, j - 1)
                    elif not is_first(s):
                        reduce(s - 1, LAST)
                    if j < LAST and UNITS[j + 1] == 2:
                        make_unit(s, UOFF[j + 1] + 1)
                    g = turn_at(s, j)
                    if g is not None:
                        pe.wait_ge(*misc_free)
                        turn(s, g)
                        misc_free = (et_ready, nth(s, g) + 1)
                    g = early_turn_at(j)
                    if g is not None and not last:
                        pe.wait_ge(*misc_free)
                        turn(s + 1, g)
                        misc_free = (et_ready, nth(s + 1, g) + 1)
                    if not is_first(s):
                        for t, k in mlp_at(j):
                            if k == 0:
                                pe.wait_ge(*misc_free)
                                misc_free = (mlp_ev, (s - 1) * NM + t + 1)
                            mlp(s - 1, t, k, misc[:])
                    if not last:
                        for g, k in lookups_at(s, j, kts):
                            if k == 0:
                                pe.wait_ge(*misc_free)
                                misc_free = (et_ready, nth(s + 1, g) + 1)
                            look_up(s + 1, g, k)
                    elif LAST - KT < j < LAST:
                        if j == LAST - KT + 1:
                            pe.wait_ge(*misc_free)
                        mlp(s, 0, j - (LAST - KT + 1), last_dst(0))

            pe.wait_ge(con_in, 16)
            for g in range(OHG):
                for k in range(kts[g]):
                    look_up(0, g, k, zbank if g else misc)
            make_unit(0, 0)
            pe.wait_ge(et_ready, OHG)
            turn(0, OHG)
            slice_steps(0)
            pe.wait_ge(w1_in, 16)
            pe.wait_ge(w2_in, 16)
            pe.wait_ge(vec_in, 16)
            with pe.Fori(1, NS - 1) as s:
                slice_steps(s)
            slice_steps(NS - 1, last=True)
            reduce(NS - 1, LAST)
            for t in range(NM):
                if t == 1:
                    pe.wait_ge(multiplied, NS * NU)
                if t > RING:
                    pe.wait_ge(mlp_ev, (NS - 1) * NM + t - RING + 1)
                for k in range(0 if t else KT - 1, MLP_K[t]):
                    mlp(NS - 1, t, k, last_dst(t))


def field_order(vocab):
    small = sorted((f for f in range(F) if vocab[f] % PV == 0), key=lambda f: (vocab[f], f))[:OHG * GS]
    return small + [f for f in range(F) if f not in small]


def pair_index(i, j):
    return i * (2 * F - i - 1) // 2 + (j - i - 1)


def lay_out_pairs(W, order):
    def mat(src, dst):
        return W[pair_index(src, dst)] if src < dst else W[pair_index(dst, src)].T

    pairs = np.zeros((NJ, D, GS, GS, D), W.dtype)
    for j, (gs, gd) in enumerate(STEPS):
        for a in range(GS):
            for b in range(GS):
                if gs != gd or any((a, b) == own[:2] for own in OWN):
                    pairs[j, :, a, b] = mat(order[gs * GS + a], order[gd * GS + b])
    return pairs.reshape(NJ * D, GS * P)


def top_rows(order):
    rows = np.zeros((P, KT), np.int64)
    for j, (gs, gd) in enumerate(STEPS):
        k, m = j // SPT, j % SPT
        for a in range(GS):
            for q in range(GS):
                if gs != gd:
                    pair = (order[gs * GS + a], order[gd * GS + q])
                elif any((q, a) == own[1:] for own in OWN):
                    source = next(own[0] for own in OWN if (q, a) == own[1:])
                    pair = (order[gs * GS + source], order[gs * GS + q])
                else:
                    continue
                rows[a * D + m * SLOT + q, k] = pair_index(min(pair), max(pair))
    for a in range(GS):
        for r in range(SLOT):
            rows[a * D + (SPT - 1) * SLOT + r, KT - 1] = F * (F - 1) // 2 + a * SLOT + r
    return rows


def constants(kts):
    KTM = max(kts)
    sel = np.zeros((P, SELW), np.float32)
    sel[np.arange(P), SELW - D + np.arange(P) // D] = 1
    dsel = np.zeros((P, GS * D), np.float32)
    for r in range(DENSE):
        dsel[r, (r // SLOT) * D + (SPT - 1) * SLOT + r % SLOT] = 1
    vcol = np.zeros((P, len(kts), KTM), np.float32)
    for g, k in enumerate(kts):
        vcol[:, g, :k] = np.arange(P)[:, None] * k + np.arange(k)
    return np.concatenate([sel, dsel, vcol.reshape(P, -1), np.eye(P, dtype=np.float32)], axis=1)


def kernel(dense_ctx, ids, W_top1, b_top1, W_top2, b_top2, W_top3, L0_rec_W, **tables):
    import numpy as _np
    import concourse.bacc as _bacc
    from concourse import mybir as _mybir
    from concourse.bass_utils import run_bass_kernel_spmd as _run

    tabs = [_np.asarray(tables[f"tbl_{f}"]) for f in range(F)]
    order = field_order([t.shape[0] for t in tabs])
    vocab = [tabs[f].shape[0] for f in order]
    kts = [vocab[g * GS] // PV for g in range(OHG)]
    idT = _np.asarray(ids).T[order]
    noh = OHG * GS
    w_pairs = lay_out_pairs(_np.asarray(L0_rec_W), order)
    arrays = {
        "ids_oh": idT[:noh].reshape(P, -1),
        "ids_g": idT[noh:].reshape(GG, GS, NS, NT, P).transpose(2, 4, 0, 3, 1),
        "ctxT": _np.asarray(dense_ctx).reshape(NS, N, DENSE).transpose(0, 2, 1),
        "w_pairs": w_pairs,
        "w1": _np.asarray(W_top1)[top_rows(order)],
        "w2": _np.asarray(W_top2).reshape(H1 // P, P, H2).transpose(1, 0, 2),
        "vecs": _np.concatenate([_np.asarray(x).reshape(-1, P).T for x in (b_top1, b_top2, W_top3)], axis=1),
        "consts": constants(kts),
    }
    for i, f in enumerate(order):
        arrays[f"table{i}"] = tabs[f]
    arrays = {k: _np.ascontiguousarray(v) for k, v in arrays.items()}

    nc = _bacc.Bacc("TRN2", target_bir_lowering=False, num_devices=1)
    ap = {k: nc.dram_tensor(k, v.shape, _mybir.dt.from_np(v.dtype), kind="ExternalInput").ap()
          for k, v in arrays.items()}
    scratch = nc.dram_tensor("scratch", (noh * B,), F16, kind="Internal").ap()
    w_parts = nc.dram_tensor("w_parts", (NJ, 2, D, GS * P), F32, kind="Internal").ap()
    out = nc.dram_tensor("y", (NS, 1, N), F32, kind="ExternalOutput").ap()
    build(nc, vocab, ap["ids_oh"], ap["ids_g"], ap["ctxT"], ap["w_pairs"], ap["w1"], ap["w2"], ap["vecs"],
          ap["consts"], [ap[f"table{i}"] for i in range(F)], scratch, w_parts, out)
    r = _run(nc, [arrays], core_ids=[0])
    return r.results[0]["y"].reshape(B, 1)
```
